# Optimizing a Trainium2 kernel written in Bass

```python
import numpy as np
import jax
import jax.numpy as jnp

def _softmax(x, axis=-1):
    return jax.nn.softmax(x, axis=axis)

def _gelu(x):
    return jax.nn.gelu(x, approximate=True)

def _silu(x):
    return jax.nn.silu(x)

def _sigmoid(x):
    return jax.nn.sigmoid(x)

def _layernorm(x, axis=-1, eps=1e-05):
    m = jnp.mean(x, axis=axis, keepdims=True)
    v = jnp.var(x, axis=axis, keepdims=True)
    return (x - m) / jnp.sqrt(v + eps)

def _scatter_add(tgt, idx, src, axis=0):
    return tgt.at[idx].add(src)

def _segment_sum(src, seg, n):
    return jax.ops.segment_sum(src, seg, n)
kernel_name = 'mk_early_fusion_d1_tok_img768_r4_c99640'

def setup_inputs(seed: int=0):
    np.random.seed(seed)
    _w = jnp.asarray

    def _rec_inputs():
        import jax
        import jax.numpy as jnp
        _rk = jax.random.key(seed)
        x = jax.random.uniform(jax.random.fold_in(_rk, 1), (16, 3, 96, 96), jnp.float32, 0.0, 1)
        txt = 0.0181629 + 1.04976 * jax.random.normal(jax.random.fold_in(_rk, 2), (16, 77, 192), jnp.float32)
        return (x, txt)
    x, txt = _rec_inputs()

    def _L0_tok_setup():
        import jax, jax.numpy as jnp
        import numpy as np
        B, C, H, W, P, D = (32, 3, 96, 96, 16, 192)
        N = H // P * (W // P)
        key = jax.random.key(seed)
        k0, k1, k2, k3 = jax.random.split(key, 4)
        x = jax.random.uniform(k0, (B, C, H, W), dtype=jnp.float32)
        proj_w = jax.random.normal(k1, (D, P * P * C), dtype=jnp.float32) * 0.02
        proj_b = jnp.zeros((D,), jnp.float32)
        cls_token = jax.random.normal(k2, (1, 1, D), dtype=jnp.float32)
        pos_embedding = jax.random.normal(k3, (1, N + 1, D), dtype=jnp.float32)
        return {'x': x, 'proj_w': proj_w, 'proj_b': proj_b, 'cls_token': cls_token, 'pos_embedding': pos_embedding}
    _L0_tok_all = _L0_tok_setup()
    _L0_tok_in = {k: v for k, v in _L0_tok_all.items() if k in ('proj_w', 'proj_b', 'cls_token', 'pos_embedding')}
    del _L0_tok_all

    def _L0_attn_setup():
        import jax, jax.numpy as jnp
        import numpy as np
        B, N, D = (64, 197, 192)
        H, E, R = (12, 8, 8)
        key = jax.random.key(seed)
        ks = jax.random.split(key, 8)
        s = 0.02
        return {'tokens': jax.random.normal(ks[0], (B, N, D), dtype=jnp.float32), 'qkv_w': jax.random.normal(ks[1], (3 * D, D), dtype=jnp.float32) * s, 'qkv_b': jax.random.normal(ks[2], (3 * D,), dtype=jnp.float32) * s, 'proj_w': jax.random.normal(ks[3], (D, D), dtype=jnp.float32) * s, 'proj_b': jax.random.normal(ks[4], (D,), dtype=jnp.float32) * s, 'gate_w': jax.random.normal(ks[5], (E, D), dtype=jnp.float32) * s, 'lora_a': jax.random.normal(ks[6], (E, D, R), dtype=jnp.float32) * s, 'lora_b': jax.random.normal(ks[7], (E, R, 3 * D), dtype=jnp.float32) * s}
    _L0_attn_all = _L0_attn_setup()
    _L0_attn_in = {k: v for k, v in _L0_attn_all.items() if k in ('qkv_w', 'qkv_b', 'proj_w', 'proj_b', 'gate_w', 'lora_a', 'lora_b')}
    del _L0_attn_all

    def _L0_ffn_setup():
        import jax, jax.numpy as jnp
        import numpy as np
        D = 192
        I = 768
        E = 8
        K = 2
        LIMIT = 10.0
        VOCAB = 8192

        def _expert(xf, W1, W2, W3):
            gate = jnp.minimum(xf @ W1, LIMIT)
            up = jnp.clip(xf @ W3, -LIMIT, LIMIT)
            return jax.nn.silu(gate) * up @ W2
        key = jax.random.key(seed)
        ks = jax.random.split(key, 10)
        s = 0.02
        return {'x': jax.random.normal(ks[0], (1, 512, D), dtype=jnp.float32), 'input_ids': jax.random.randint(ks[1], (1, 512), 0, VOCAB, dtype=jnp.int64), 'gate_w': jax.random.normal(ks[2], (D, E), dtype=jnp.float32) * s, 'gate_bias': jnp.zeros((E,), dtype=jnp.float32), 'w1': jax.random.normal(ks[3], (E, D, I), dtype=jnp.float32) * s, 'w2': jax.random.normal(ks[4], (E, I, D), dtype=jnp.float32) * s, 'w3': jax.random.normal(ks[5], (E, D, I), dtype=jnp.float32) * s, 'w1s': jax.random.normal(ks[6], (D, I), dtype=jnp.float32) * s, 'w2s': jax.random.normal(ks[7], (I, D), dtype=jnp.float32) * s, 'w3s': jax.random.normal(ks[8], (D, I), dtype=jnp.float32) * s}
    _L0_ffn_all = _L0_ffn_setup()
    _L0_ffn_in = {k: v for k, v in _L0_ffn_all.items() if k in ('input_ids', 'gate_w', 'gate_bias', 'w1', 'w2', 'w3', 'w1s', 'w2s', 'w3s')}
    del _L0_ffn_all
    return {'x': x, 'txt': txt, 'L0_tok_proj_w': _L0_tok_in['proj_w'], 'L0_tok_proj_b': _L0_tok_in['proj_b'], 'L0_tok_cls_token': _L0_tok_in['cls_token'], 'L0_tok_pos_embedding': _L0_tok_in['pos_embedding'], 'L0_attn_qkv_w': _L0_attn_in['qkv_w'], 'L0_attn_qkv_b': _L0_attn_in['qkv_b'], 'L0_attn_proj_w': _L0_attn_in['proj_w'], 'L0_attn_proj_b': _L0_attn_in['proj_b'], 'L0_attn_gate_w': _L0_attn_in['gate_w'], 'L0_attn_lora_a': _L0_attn_in['lora_a'], 'L0_attn_lora_b': _L0_attn_in['lora_b'], 'L0_ffn_input_ids': _L0_ffn_in['input_ids'], 'L0_ffn_gate_w': _L0_ffn_in['gate_w'], 'L0_ffn_gate_bias': _L0_ffn_in['gate_bias'], 'L0_ffn_w1': _L0_ffn_in['w1'], 'L0_ffn_w2': _L0_ffn_in['w2'], 'L0_ffn_w3': _L0_ffn_in['w3'], 'L0_ffn_w1s': _L0_ffn_in['w1s'], 'L0_ffn_w2s': _L0_ffn_in['w2s'], 'L0_ffn_w3s': _L0_ffn_in['w3s']}

def reference(x, txt, L0_tok_proj_w, L0_tok_proj_b, L0_tok_cls_token, L0_tok_pos_embedding, L0_attn_qkv_w, L0_attn_qkv_b, L0_attn_proj_w, L0_attn_proj_b, L0_attn_gate_w, L0_attn_lora_a, L0_attn_lora_b, L0_ffn_input_ids, L0_ffn_gate_w, L0_ffn_gate_bias, L0_ffn_w1, L0_ffn_w2, L0_ffn_w3, L0_ffn_w1s, L0_ffn_w2s, L0_ffn_w3s):
    import jax
    import jax.numpy as jnp

    def _L0_tok_ref(x, proj_w, proj_b, cls_token, pos_embedding):
        import jax, jax.numpy as jnp
        import numpy as np
        B, C, H, W, P, D = (32, 3, 96, 96, 16, 192)
        N = H // P * (W // P)
        b, c, h, w = x.shape
        hp, wp = (h // P, w // P)
        patches = x.reshape(b, c, hp, P, wp, P).transpose(0, 2, 4, 1, 3, 5).reshape(b, hp * wp, c * P * P)
        tok = jnp.einsum('bnk,dk->bnd', patches, proj_w) + proj_b
        cls = jnp.broadcast_to(cls_token, (b, 1, cls_token.shape[-1]))
        z0 = jnp.concatenate([cls, tok], axis=1) + pos_embedding
        return z0

    def _L0_attn_ref(tokens, qkv_w, qkv_b, proj_w, proj_b, gate_w, lora_a, lora_b):
        import jax, jax.numpy as jnp
        import numpy as np
        B, N, D = (64, 197, 192)
        H, E, R = (12, 8, 8)
        b, n, d = tokens.shape
        hd = d // H
        scale = hd ** (-0.5)
        qkv = jnp.einsum('bnd,kd->bnk', tokens, qkv_w) + qkv_b
        gates = jax.nn.softmax(jnp.einsum('bnd,ed->bne', tokens, gate_w), axis=-1)
        h = jnp.einsum('bnd,edr->bner', tokens, lora_a)
        delta = jnp.einsum('bner,erk,bne->bnk', h, lora_b, gates)
        qkv = (qkv + delta).reshape(b, n, 3, H, hd).transpose(2, 0, 3, 1, 4)
        q, k, v = (qkv[0], qkv[1], qkv[2])
        attn = jax.nn.softmax(jnp.einsum('bhqd,bhkd->bhqk', q, k) * scale, axis=-1)
        out = jnp.einsum('bhqk,bhkd->bhqd', attn, v)
        out = out.transpose(0, 2, 1, 3).reshape(b, n, d)
        return jnp.einsum('bnd,kd->bnk', out, proj_w) + proj_b

    def _L0_ffn_ref(x, input_ids, gate_w, gate_bias, w1, w2, w3, w1s, w2s, w3s):
        import jax, jax.numpy as jnp
        import numpy as np
        D = 192
        I = 768
        E = 8
        K = 2
        LIMIT = 10.0
        VOCAB = 8192

        def _expert(xf, W1, W2, W3):
            gate = jnp.minimum(xf @ W1, LIMIT)
            up = jnp.clip(xf @ W3, -LIMIT, LIMIT)
            return jax.nn.silu(gate) * up @ W2
        B, T, _ = x.shape
        flat = x.reshape(-1, D)
        N = flat.shape[0]
        scores = jnp.sqrt(jax.nn.softplus(flat @ gate_w))
        routed_scores = scores + gate_bias
        _, indices = jax.lax.top_k(routed_scores, K)
        weights = jnp.take_along_axis(scores, indices, axis=1)
        weights = weights / jnp.clip(weights.sum(axis=-1, keepdims=True), 1e-06)
        combine = jnp.zeros((N, E), dtype=weights.dtype)
        combine = combine.at[jnp.arange(N)[:, None], indices].add(weights)
        y = _expert(flat, w1s, w2s, w3s)
        gate_h = jnp.minimum(jnp.einsum('td,edi->eti', flat, w1), LIMIT)
        up_h = jnp.clip(jnp.einsum('td,edi->eti', flat, w3), -LIMIT, LIMIT)
        h = jax.nn.silu(gate_h) * up_h
        out_e = jnp.einsum('eti,eid->etd', h, w2)
        routed = jnp.einsum('etd,te->td', out_e, combine)
        return (y + routed).reshape(B, T, D)
    h = _L0_tok_ref(x, L0_tok_proj_w, L0_tok_proj_b, L0_tok_cls_token, L0_tok_pos_embedding)
    h = jnp.concatenate([h, txt], axis=1)
    h = h + _L0_attn_ref(_layernorm(h, axis=-1), L0_attn_qkv_w, L0_attn_qkv_b, L0_attn_proj_w, L0_attn_proj_b, L0_attn_gate_w, L0_attn_lora_a, L0_attn_lora_b)
    h = h + _L0_ffn_ref(_layernorm(h, axis=-1), L0_ffn_input_ids, L0_ffn_gate_w, L0_ffn_gate_bias, L0_ffn_w1, L0_ffn_w2, L0_ffn_w3, L0_ffn_w1s, L0_ffn_w2s, L0_ffn_w3s)
    return h

_drawn_inputs = setup_inputs


def setup_inputs(seed=0):
    import zlib

    import numpy as np

    out = dict(_drawn_inputs(seed))
    spreads = {'L0_tok_proj_b': (0.0, 0.1), 'L0_ffn_gate_bias': (0.0, 0.559)}
    factors = {'L0_attn_qkv_w': 5.704,
     'L0_attn_qkv_b': 8.0,
     'L0_attn_proj_w': 5.236,
     'L0_attn_proj_b': 3.081,
     'L0_attn_gate_w': 8.0,
     'L0_attn_lora_a': 8.0,
     'L0_attn_lora_b': 8.0,
     'L0_ffn_gate_w': 5.74,
     'L0_ffn_w1': 3.889,
     'L0_ffn_w2': 3.854,
     'L0_ffn_w3': 3.86,
     'L0_ffn_w1s': 2.756,
     'L0_ffn_w2s': 2.75,
     'L0_ffn_w3s': 2.73}
    for name, (base, spread) in spreads.items():
        noise = np.random.default_rng([zlib.crc32(name.encode()), seed]).standard_normal(out[name].shape)
        drawn = base * np.exp(spread * noise) if base else spread * noise
        out[name] = jnp.asarray(drawn.astype(out[name].dtype))
    for name, factor in factors.items():
        out[name] = (out[name] * factor).astype(out[name].dtype)
    return out
```

```python
from contextlib import ExitStack

import concourse.bass as bass
from concourse import mybir

F32 = mybir.dt.float32
U32 = mybir.dt.uint32
I32 = mybir.dt.int32
ALU = mybir.AluOpType
ACT = mybir.ActivationFunctionType
AX = mybir.AxisListType

B, NPATCH, NTXT, D = 16, 36, 77, 192
NEMB = NPATCH + 1
N = NEMB + NTXT
T = B * N
KP = 768
H, HD, NG, NJ = 12, 16, 3, 4
E, R, I = 8, 8, 768
DC = D // 2
LIMIT = 10.0
SILU_LIMIT = 9.999546021312976
EPS = 1e-5
SCALE = HD ** -0.5
QG = NG * 128
QOFF, KOFF, VOFF, LOFF = 0, QG, 2 * QG, 2 * QG + D
NLG = E * R + E
NWA = LOFF + NLG
VW = HD + 1

P = 128
SH_TILES = -(-T // P)
RT_TILES = (2 * T + E * (P - 1)) // P
TILES = SH_TILES + RT_TILES
XT_TILES = TILES + 1
ROW = D + 2
ID, WT = D, D + 1
HALF = I // 2
KH = HALF // P
LATE = 4

C_ID, C_TRI, C_ONE, C_IOTA = 0, 128, 242, 356
C_J = C_IOTA + B * E
C_T = C_J + E * SH_TILES
C_POW = C_T + (RT_TILES + 1) * E
C_TOK = C_POW + 16
C_FILL = C_TOK + B
C_BIAS = C_FILL + 1
C_ALL = C_BIAS + E


def program(nc, patches, txt, proj_w, mask2, cls_b, pos, wa, lora_b, out_w, gate_w, consts, w1, w2, w3, w1s, w2s, w3s, acc, xs):
    with ExitStack() as ctx:
        def sb(name, shape, dt=F32):
            return ctx.enter_context(nc.sbuf_tensor(name, shape, dt))

        def sem(name):
            return ctx.enter_context(nc.semaphore(name))

        w13 = sb("w13", [P, E + 1, 2 * 2 * I])
        wdn = sb("wdn", [P, E + 1, (I // P) * D])
        first_late = E + 1 - LATE
        late13 = w13[:, first_late:, :].rearrange("p a b -> p (a b)")
        late2 = wdn[:, first_late:, :].rearrange("p a b -> p (a b)")
        prob_sz = H * N
        prob = [late13[0:N, s * prob_sz:(s + 1) * prob_sz] for s in range(2)]
        probT = [late13[0:N, (2 + s) * prob_sz:(3 + s) * prob_sz] for s in range(2)]
        at13 = 4 * prob_sz
        qT = [late13[:, at13 + k * NG * N:at13 + (k + 1) * NG * N] for k in range(2)]
        kT = [late13[:, at13 + k * NG * N:at13 + (k + 1) * NG * N] for k in range(2, 4)]
        at13 += 4 * NG * N
        patch = [late13[:, at13 + s * 6 * NEMB:at13 + (s + 1) * 6 * NEMB].rearrange("p (k m) -> p k m", k=6) for s in range(2)]
        at13 += 12 * NEMB
        xnT = [late13[0:DC + 1, at13 + k * 2 * N:at13 + (k + 1) * 2 * N].rearrange("p (c n) -> p c n", c=2) for k in range(2)]
        oT = [late13[0:DC + 1, at13 + k * 2 * N:at13 + (k + 1) * 2 * N].rearrange("p (c n) -> p c n", c=2) for k in range(2, 4)]
        at13 += 8 * N
        assert at13 <= LATE * 4 * I
        wa_sb = late2[0:DC + 1, 0:2 * NWA].rearrange("p (c n) -> p c n", c=2)
        lb_sb = late2[0:E * R, 2 * NWA:2 * NWA + LOFF]
        ow_sb = late2[0:DC + 1, 2 * NWA + LOFF:2 * NWA + LOFF + 2 * D].rearrange("p (c n) -> p c n", c=2)
        pw_sb = late2[:, 2 * NWA + LOFF + 2 * D:2 * NWA + LOFF + 8 * D].rearrange("p (k d) -> p k d", k=6)
        assert 2 * NWA + LOFF + 8 * D <= LATE * (I // P) * D

        cst = sb("cst", [P, C_ALL])
        mask2_sb = sb("mask2_sb", [2, NEMB])
        clsb_sb = sb("clsb_sb", [2, D])
        base = sb("base", [NEMB, D])
        gw_sb = sb("gw_sb", [DC, 2, E])
        rows = sb("rows", [N, B, ROW])
        filler = sb("filler", [P, ROW])
        x2 = [sb(f"x2{s}", [N, D]) for s in range(2)]
        h = [sb(f"h{s}", [N, D]) for s in range(2)]
        xn = [sb(f"xn{s}", [N, D]) for s in range(2)]
        st = [sb(f"st{s}", [N, 32]) for s in range(2)]
        hg = [sb(f"hg{s}", [N, E * R + 3 * E]) for s in range(2)]
        hgT = [sb(f"hgT{s}", [E * R, N]) for s in range(2)]
        va = [sb(f"va{s}", [N, H, VW]) for s in range(2)]
        smx = [sb(f"smx{s}", [N, 2 * H]) for s in range(2)]
        o = [sb(f"o{s}", [N, D]) for s in range(2)]
        x2T = [sb(f"x2T{s}", [DC, 2, N]) for s in range(2)]
        logit = sb("logit", [N, B, E])
        rt = sb("rt", [N, 14, B * E])
        rs = sb("rs", [N, 12, B])
        off = sb("off", [N, 6, E])
        jcmp = sb("jcmp", [N, E * SH_TILES])
        slot1 = sb("slot1", [N, B], U32)
        slot2 = sb("slot2", [N, B], U32)
        etab = sb("etab", [N, XT_TILES], I32)

        xin = [sb(f"xin{s}", [P, ROW]) for s in range(2)]
        xT = [sb(f"xT{s}", [DC, 2, P]) for s in range(2)]
        meta = sb("meta", [P, XT_TILES, 2])
        gbuf = [sb(f"gbuf{i}", [P, HALF]) for i in range(2)]
        ubuf = [sb(f"ubuf{i}", [P, HALF]) for i in range(2)]
        hbuf = [sb(f"hbuf{i}", [P, HALF]) for i in range(2)]
        hT = [sb(f"hT{i}", [P, KH, P]) for i in range(2)]
        yout = [sb(f"yout{s}", [P, D]) for s in range(2)]
        idx = [sb(f"idx{s}", [P, 1], U32) for s in range(2)]

        ps = ctx.enter_context(nc.psum_tensor("ps", [P, 8, 512], F32))
        ident = cst[:, C_ID:C_ID + P]

        def bank(s, b):
            return ps[:, 4 * s + b, :]

        const_in, wa_in, w_shared, w_routed = sem("const_in"), sem("wa_in"), sem("w_shared"), sem("w_routed")
        txt_in = [sem(f"txt_in{s}") for s in range(2)]
        patch_in = [sem(f"patch_in{s}") for s in range(2)]
        E_ps, xnT_ps, lora_ps, hgT_ps = sem("E_ps"), sem("xnT_ps"), sem("lora_ps"), sem("hgT_ps")
        q_ps, k_ps, v_ps, s_ps = sem("q_ps"), sem("k_ps"), sem("v_ps"), sem("s_ps")
        pT_ps, pv_ps, oT_ps, proj_ps = sem("pT_ps"), sem("pv_ps"), sem("oT_ps"), sem("proj_ps")
        x2T_ps, logit_ps, base_ps = sem("x2T_ps"), sem("logit_ps"), sem("base_ps")
        base_done, ones_done = sem("base_done"), sem("ones_done")
        h_sum, bn1, mv1, xn_done = sem("h_sum"), sem("bn1"), sem("mv1"), sem("xn_done")
        veps, rstd1, rstd2 = sem("veps"), sem("rstd1"), sem("rstd2")
        gmax, gexp, grcp, hg_done = sem("gmax"), sem("gexp"), sem("grcp"), sem("hg_done")
        xnT_done, hgT_done, q_done, k_done, v_done = (sem(x) for x in ("xnT_done", "hgT_done", "q_done", "k_done", "v_done"))
        smax, ssub, p_done, pT_done = sem("smax"), sem("ssub"), sem("p_done"), sem("pT_done")
        ssum, o_done, oT_done, h2_done = sem("ssum"), sem("o_done"), sem("oT_done"), sem("h2_done")
        bn2, mv2, x2_done, x2T_done, logit_done = (sem(x) for x in ("bn2", "mv2", "x2_done", "x2T_done", "logit_done"))
        row_done = sem("row_done")
        h2_out = [sem(f"h2_out{s}") for s in range(2)]
        x2_out = sem("x2_out")
        fill_done, fill_out = sem("fill_done"), sem("fill_out")
        rstep, absl, uexp, lnw, softp, root = (sem(x) for x in ("rstep", "absl", "uexp", "lnw", "softp", "root"))
        picks, rank_ps, rank_copied, slots, w1_set, w2_set = (sem(x) for x in ("picks", "rank_ps", "rank_copied", "slots", "w1_set", "w2_set"))
        scat1, scat2 = sem("scat1"), sem("scat2")
        x_in = [sem(f"x_in{s}") for s in range(2)]
        xT_ps, xT_done, meta_done = sem("xT_ps"), sem("xT_done"), sem("meta_done")
        g_ps, u_ps, silu_done, clip_done, hh_done = (sem(x) for x in ("g_ps", "u_ps", "silu_done", "clip_done", "hh_done"))
        hT_ps, hT_done, y_ps, y_done, idx_done, y_out = (sem(x) for x in ("hT_ps", "hT_done", "y_ps", "y_done", "idx_done", "y_out"))

        block = ctx.enter_context(nc.Block())

        @block.sync
        def _(sp):
            def load_txt(n, s):
                sp.dma_start(h[s][NEMB:N, :], txt[bass.ds(n, 1)].rearrange("a t d -> (a t) d")).then_inc(txt_in[s], 16)

            def load_patches(n, s):
                sp.dma_start(patch[s][:, :, :], patches[bass.ds(n, 1)].rearrange("a p k m -> (a p) k m"))\
                    .then_inc(patch_in[s], 16)

            sp.dma_start(cst[:, :], consts[:, :]).then_inc(const_in, 16)
            sp.dma_start(mask2_sb[:, :], mask2[:, :]).then_inc(const_in, 16)
            sp.dma_start(clsb_sb[:, :], cls_b[:, :]).then_inc(const_in, 16)
            sp.dma_start(base[:, :], pos[:, :]).then_inc(const_in, 16)
            sp.dma_start(pw_sb[:, :, :], proj_w[:, :, :]).then_inc(const_in, 16)
            for n in range(2):
                load_patches(n, n)
                load_txt(n, n)
            sp.dma_start(gw_sb[:, :, :], gate_w[:, :, :]).then_inc(wa_in, 16)
            sp.dma_start(wa_sb, wa[:, :, :]).then_inc(wa_in, 16)
            sp.dma_start(lb_sb, lora_b[:, :]).then_inc(wa_in, 16)
            sp.dma_start(ow_sb, out_w[:, :, :]).then_inc(wa_in, 16)
            sp.wait_ge(fill_done, 3)
            sp.dma_start(xs[T:SH_TILES * P, :], filler[P - (SH_TILES * P - T):P, :]).then_inc(fill_out, 16)
            sp.dma_start(xs[SH_TILES * P:XT_TILES * P, :].rearrange("(t p) c -> p t c", p=P),
                         filler[:, :].unsqueeze(1).broadcast_to([P, XT_TILES - SH_TILES, ROW])).then_inc(fill_out, 16)
            sp.dma_start(acc[T:T + P, :], filler[:, 0:D]).then_inc(fill_out, 16)

            def store_tile(n, s):
                sp.wait_ge(h2_done, n + 1)
                sp.dma_start(acc[bass.ds(n * N, N), :], h[s][:, :]).then_inc(h2_out[s], 16)
                sp.wait_ge(row_done, n + 1)
                sp.dma_start(xs[bass.ds(n * N, N), :], rows[:, bass.ds(n, 1), :].rearrange("p a c -> p (a c)"))\
                    .then_inc(x2_out, 16)

            def refill_tile(n, s, times):
                sp.wait_ge(E_ps, n - 1)
                load_patches(n, s)
                sp.wait_ge(h2_out[s], times)
                load_txt(n, s)

            for n in range(2):
                store_tile(n, n)
                refill_tile(n + 2, n, 16)
            with sp.Fori(1, B // 2 - 1) as i:
                for s in range(2):
                    store_tile(2 * i + s, s)
                    refill_tile(2 * i + s + 2, s, 16 * i + 16)
            for n in range(B - 2, B):
                store_tile(n, n % 2)

            def load_slots(t, s, times):
                if times is not None:
                    sp.wait_ge(xT_ps, t - 1)
                    sp.wait_ge(meta_done, t - 1)
                sp.dma_start(xin[s][:, :], xs[bass.ds(t * P, P), :]).then_inc(x_in[s], 16)

            sp.wait_ge(x2_out, 16 * B)
            sp.wait_ge(fill_out, 48)
            sp.wait_ge(w_shared, 48)
            load_slots(0, 0, None)
            load_slots(1, 1, None)
            with sp.Fori(1, SH_TILES // 2) as i:
                for s in range(2):
                    load_slots(2 * i + s, s, i)
            load_slots(SH_TILES - 1, 0, 0)
            sp.wait_ge(scat2, 16 * B)
            sp.wait_ge(scat1, 16 * B)
            sp.wait_ge(w_routed, 48 * E)
            sp.wait_ge(h2_out[0], 8 * B)
            sp.wait_ge(h2_out[1], 8 * B)
            load_slots(SH_TILES, 1, 0)
            with sp.Fori(SH_TILES // 2 + 1, XT_TILES // 2) as i:
                for s in range(2):
                    load_slots(2 * i + s, s, i)
            sp.wait_ge(x_in[0], 8 * XT_TILES)
            sp.wait_ge(x_in[1], 8 * XT_TILES)
            sp.wait_ge(y_out, 16 * TILES)

        @block.tensor
        def _(pe):
            mm = nc.tensor.matmul

            def embed(n, s, times):
                pe.wait_ge(patch_in[s], times)
                for k in range(6):
                    last = mm(bank(s, 0)[0:NEMB, 0:D], patch[s][:, k, :], pw_sb[:, k, :],
                              start=(k == 0), stop=(k == 5))
                last.then_inc(E_ps, 1)

            def transpose_x(n, s):
                pe.wait_ge(xn_done, n + 1)
                for c in range(2):
                    last = nc.tensor.transpose(bank(s, 1)[0:DC, c * N:(c + 1) * N], xn[s][:, c * DC:(c + 1) * DC],
                                               ident[0:N, 0:N])
                last.then_inc(xnT_ps, 1)

            def lora_down(n, s):
                pe.wait_ge(xnT_done, n + 1)
                for c in range(2):
                    last = mm(bank(s, 2)[0:N, 0:NLG], xnT[s][0:DC, c, :], wa_sb[0:DC, c, LOFF:NWA],
                              start=(c == 0), stop=(c == 1))
                last.then_inc(lora_ps, 1)

            def transpose_hg(n, s):
                pe.wait_ge(hg_done, n + 1)
                nc.tensor.transpose(bank(s, 1)[0:NLG, 0:N], hg[s][:, 0:NLG], ident[0:N, 0:N]).then_inc(hgT_ps, 1)

            def qkv(n, s):
                pe.wait_ge(hgT_done, n + 1)
                for off0, b, done in ((QOFF, 0, q_ps), (KOFF, 1, k_ps)):
                    for g in range(NG):
                        cols = slice(off0 + g * P, off0 + (g + 1) * P)
                        out = bank(s, b)[:, g * N:(g + 1) * N]
                        mm(out, wa_sb[0:DC, 0, cols], xnT[s][0:DC, 0, :], start=True, stop=False)
                        mm(out, wa_sb[0:DC + 1, 1, cols], xnT[s][0:DC + 1, 1, :], start=False, stop=False)
                        last = mm(out, lb_sb[:, cols], hgT[s][:, :], start=False, stop=True)
                    last.then_inc(done, 1)
                out = bank(s, 3)[0:N, 0:D]
                mm(out, xnT[s][0:DC, 0, :], wa_sb[0:DC, 0, VOFF:LOFF], start=True, stop=False)
                mm(out, xnT[s][0:DC + 1, 1, :], wa_sb[0:DC + 1, 1, VOFF:LOFF], start=False, stop=False)
                mm(out, hgT[s][:, :], lb_sb[:, VOFF:LOFF], start=False, stop=True).then_inc(v_ps, 1)

            def scores(n, s):
                pe.wait_ge(q_done, n + 1)
                pe.wait_ge(k_done, n + 1)
                pe.wait_ge(v_done, n + 1)
                for g in range(NG):
                    for j in range(NJ):
                        at = slice(32 * j, 32 * j + HD)
                        last = mm(bank(s, j)[0:N, g * N:(g + 1) * N], qT[s][at, g * N:(g + 1) * N],
                                  kT[s][at, g * N:(g + 1) * N], start=True, stop=True)
                last.then_inc(s_ps, 1)

            def transpose_p(n, s):
                pe.wait_ge(p_done, n + 1)
                for a in range(H):
                    last = nc.tensor.transpose(bank(s, a // 4)[0:N, (a % 4) * N:(a % 4 + 1) * N],
                                               prob[s][:, a * N:(a + 1) * N], ident[0:N, 0:N])
                    if a % 4 == 3:
                        last.then_inc(pT_ps, 1)

            def weigh_v(n, s):
                pe.wait_ge(pT_done, 3 * n + 3)
                for a in range(H):
                    head = NJ * (a % NG) + a // NG
                    last = mm(bank(s, 3)[0:N, head * VW:(head + 1) * VW], probT[s][:, a * N:(a + 1) * N],
                              va[s][:, head, :], start=True, stop=True)
                last.then_inc(pv_ps, 1)

            def transpose_o(n, s):
                pe.wait_ge(o_done, n + 1)
                for c in range(2):
                    last = nc.tensor.transpose(bank(s, 0)[0:DC, c * N:(c + 1) * N], o[s][:, c * DC:(c + 1) * DC],
                                               ident[0:N, 0:N])
                last.then_inc(oT_ps, 1)

            def project(n, s):
                pe.wait_ge(oT_done, n + 1)
                out = bank(s, 1)[0:N, 0:D]
                mm(out, oT[s][0:DC, 0, :], ow_sb[0:DC, 0, :], start=True, stop=False)
                mm(out, oT[s][0:DC + 1, 1, :], ow_sb[0:DC + 1, 1, :], start=False, stop=True).then_inc(proj_ps, 1)

            def transpose_x2(n, s):
                pe.wait_ge(x2_done, n + 1)
                for c in range(2):
                    last = nc.tensor.transpose(bank(s, 2)[0:DC, c * N:(c + 1) * N], x2[s][:, c * DC:(c + 1) * DC],
                                               ident[0:N, 0:N])
                last.then_inc(x2T_ps, 1)

            def route(n, s):
                pe.wait_ge(x2T_done, n + 1)
                for c in range(2):
                    last = mm(bank(s, 3)[0:N, 0:E], x2T[s][:, c, :], gw_sb[:, c, :], start=(c == 0), stop=(c == 1))
                last.then_inc(logit_ps, 1)

            def pair(n, s, before, after, times):
                z = 1 - s
                scores(n, s)
                if before:
                    transpose_x2(n - 1, z)
                    route(n - 1, z)
                if after:
                    embed(n + 1, z, times)
                transpose_p(n, s)
                if after:
                    transpose_x(n + 1, z)
                    lora_down(n + 1, z)
                weigh_v(n, s)
                if after:
                    transpose_hg(n + 1, z)
                transpose_o(n, s)
                if after:
                    qkv(n + 1, z)
                project(n, s)

            pe.wait_ge(const_in, 80)
            mm(bank(1, 3)[0:NEMB, 0:D], mask2_sb[:, :], clsb_sb[:, :], start=True, stop=True).then_inc(base_ps, 1)
            embed(0, 0, 16)
            pe.wait_ge(wa_in, 64)
            pe.wait_ge(ones_done, 8)
            transpose_x(0, 0)
            lora_down(0, 0)
            transpose_hg(0, 0)
            pe.wait_ge(base_done, 1)
            qkv(0, 0)
            pair(0, 0, False, True, 16)
            pair(1, 1, True, True, 32)
            with pe.Fori(1, B // 2 - 1) as i:
                pair(2 * i, 0, True, True, 16 * i + 16)
                pair(2 * i + 1, 1, True, True, 16 * i + 32)
            pair(B - 2, 0, True, True, 8 * B)
            pair(B - 1, 1, True, False, None)
            transpose_x2(B - 1, 1)
            route(B - 1, 1)

            pe.wait_ge(picks, 1)
            mm(bank(0, 0)[0:N, 0:B * E], cst[0:N, C_TRI:C_TRI + N], rt[:, PICK, :], start=True, stop=True)
            mm(bank(0, 1)[0:N, 0:B * E], cst[0:N, C_ONE:C_ONE + N], rt[:, PICK, :], start=True, stop=True)\
                .then_inc(rank_ps, 1)
            pe.wait_ge(rank_copied, 1)

            def x_transpose(t, s, times):
                pe.wait_ge(x_in[s], times)
                for c in range(2):
                    last = nc.tensor.transpose(ps[0:DC, 7, c * P:(c + 1) * P], xin[s][:, c * DC:(c + 1) * DC], ident)
                last.then_inc(xT_ps, 1)

            def gate(e, s, half):
                for c in range(2):
                    last = mm(ps[:, half, 0:HALF], xT[s][:, c, :],
                              w13[0:DC, e, c * 2 * I + half * HALF:c * 2 * I + (half + 1) * HALF],
                              start=(c == 0), stop=(c == 1))
                last.then_inc(g_ps, 1)

            def up(e, s, half):
                for c in range(2):
                    last = mm(ps[:, 2 + half, 0:HALF], xT[s][:, c, :],
                              w13[0:DC, e, c * 2 * I + I + half * HALF:c * 2 * I + I + (half + 1) * HALF],
                              start=(c == 0), stop=(c == 1))
                last.then_inc(u_ps, 1)

            def h_transpose(t, half):
                pe.wait_ge(hh_done, 2 * t + half + 1)
                for k in range(KH):
                    last = nc.tensor.transpose(ps[:, 4 + half, k * P:(k + 1) * P], hbuf[half][:, k * P:(k + 1) * P], ident)
                last.then_inc(hT_ps, 1)

            def down(t, e, half):
                pe.wait_ge(hT_done, 2 * t + half + 1)
                if half == 0:
                    if not (isinstance(t, int) and t == 0):
                        pe.wait_ge(y_done, t)
                for k in range(KH):
                    kk = half * KH + k
                    last = mm(ps[:, 6, 0:D], hT[half][:, k, :], wdn[:, e, kk * D:(kk + 1) * D],
                              start=(kk == 0), stop=(kk == I // P - 1))
                if half == 1:
                    last.then_inc(y_ps, 1)

            def tile(t, s, times):
                e = pe.value_load(etab[0:1, bass.ds(t, 1)], min_val=0, max_val=E)
                e_before = pe.value_load(etab[0:1, bass.ds(t - 1, 1)], min_val=0, max_val=E)
                pe.wait_ge(xT_done, t + 1)
                gate(e, s, 0)
                h_transpose(t - 1, 1)
                up(e, s, 0)
                down(t - 1, e_before, 1)
                x_transpose(t + 1, 1 - s, times)
                gate(e, s, 1)
                h_transpose(t, 0)
                up(e, s, 1)
                down(t, e, 0)

            x_transpose(0, 0, 16)
            pe.wait_ge(xT_done, 1)
            gate(0, 0, 0)
            up(0, 0, 0)
            x_transpose(1, 1, 16)
            gate(0, 0, 1)
            h_transpose(0, 0)
            up(0, 0, 1)
            down(0, 0, 0)
            with pe.Fori(0, (TILES - 1) // 2) as i:
                tile(2 * i + 1, 1, 16 * i + 32)
                tile(2 * i + 2, 0, 16 * i + 32)
            e_last = pe.value_load(etab[0:1, TILES - 1:TILES], min_val=0, max_val=E)
            h_transpose(TILES - 1, 1)
            down(TILES - 1, e_last, 1)

        @block.scalar
        def _(act):
            cp = nc.scalar.copy
            act.wait_ge(wa_in, 64)
            act.wait_ge(patch_in[1], 16)
            for src, at in ((w1s, 0), (w3s, I)):
                act.dma_start(w13[0:DC, 0, :].rearrange("p (c m) -> p c m", c=2)[:, :, at:at + I],
                              src.rearrange("(c p) i -> p c i", c=2)).then_inc(w_shared, 16)
            act.dma_start(wdn[:, 0, :].rearrange("p (k d) -> p k d", d=D),
                          w2s.rearrange("(k p) d -> p k d", p=P)).then_inc(w_shared, 16)

            def load_expert(e):
                for src, at in ((w1, 0), (w3, I)):
                    act.dma_start(w13[0:DC, bass.ds(e + 1, 1), :].rearrange("p a (c m) -> p (a c) m", c=2)[:, :, at:at + I],
                                  src[bass.ds(e, 1)].rearrange("a (c p) i -> p (a c) i", c=2)).then_inc(w_routed, 16)
                act.dma_start(wdn[:, bass.ds(e + 1, 1), :].rearrange("p a (k d) -> p (a k) d", d=D),
                              w2[bass.ds(e, 1)].rearrange("a (k p) d -> p (a k) d", p=P)).then_inc(w_routed, 16)

            with act.Fori(0, E - LATE) as e:
                load_expert(e)

            def xnT_copy(n, s):
                act.wait_ge(xnT_ps, n + 1)
                cp(xnT[s][0:DC, :, :].rearrange("p c n -> p (c n)"), bank(s, 1)[0:DC, 0:2 * N]).then_inc(xnT_done, 1)

            def gate_exp(n, s):
                act.wait_ge(gmax, n + 1)
                nc.scalar.activation(hg[s][:, E * R:E * R + E], bank(s, 2)[0:N, E * R:NLG], ACT.Exp,
                                     bias=st[s][:, 16:17], accum_out=st[s][:, 17:18]).then_inc(gexp, 1)

            def hgT_copy(n, s):
                act.wait_ge(hgT_ps, n + 1)
                cp(hgT[s][:, :], bank(s, 1)[0:E * R, 0:N]).then_inc(hgT_done, 1)

            def qkv_copy(n, s):
                act.wait_ge(q_ps, n + 1)
                cp(qT[s][:, :], bank(s, 0)[:, 0:NG * N]).then_inc(q_done, 1)
                act.wait_ge(k_ps, n + 1)
                cp(kT[s][:, :], bank(s, 1)[:, 0:NG * N]).then_inc(k_done, 1)
                act.wait_ge(v_ps, n + 1)
                cp(va[s][:, :, 0:HD], bank(s, 3)[0:N, 0:D].rearrange("p (h d) -> p h d", d=HD)).then_inc(v_done, 1)

            def p_exp(n, s):
                act.wait_ge(ssub, n + 1)
                nc.scalar.activation(prob[s], prob[s], ACT.Exp, scale=SCALE).then_inc(p_done, 1)

            def pT_copy(n, s):
                for b in range(3):
                    act.wait_ge(pT_ps, 3 * n + b + 1)
                    cp(probT[s][:, 4 * b * N:4 * (b + 1) * N], bank(s, b)[0:N, 0:4 * N]).then_inc(pT_done, 1)

            def oT_copy(n, s):
                act.wait_ge(oT_ps, n + 1)
                cp(oT[s][0:DC, :, :].rearrange("p c n -> p (c n)"), bank(s, 0)[0:DC, 0:2 * N]).then_inc(oT_done, 1)

            def x2T_copy(n, s):
                act.wait_ge(x2T_ps, n + 1)
                cp(x2T[s][:, :, :].rearrange("p c n -> p (c n)"), bank(s, 2)[0:DC, 0:2 * N]).then_inc(x2T_done, 1)

            def pair(n, s, before, after):
                z = 1 - s
                if before:
                    x2T_copy(n - 1, z)
                p_exp(n, s)
                pT_copy(n, s)
                if after:
                    xnT_copy(n + 1, z)
                    gate_exp(n + 1, z)
                    hgT_copy(n + 1, z)
                oT_copy(n, s)
                if after:
                    qkv_copy(n + 1, z)

            xnT_copy(0, 0)
            gate_exp(0, 0)
            hgT_copy(0, 0)
            qkv_copy(0, 0)
            pair(0, 0, False, True)
            pair(1, 1, True, True)
            with act.Fori(1, B // 2 - 1) as i:
                pair(2 * i, 0, True, True)
                pair(2 * i + 1, 1, True, True)
            pair(B - 2, 0, True, True)
            pair(B - 1, 1, True, False)
            x2T_copy(B - 1, 1)
            act.wait_ge(proj_ps, B)
            with act.Fori(E - LATE, E) as e:
                load_expert(e)

            act.wait_ge(absl, 1)
            nc.scalar.activation(rt[:, U_, :], rt[:, ABS_, :], ACT.Exp, scale=-1.0).then_inc(uexp, 1)
            act.wait_ge(uexp, 1)
            nc.scalar.activation(rt[:, LNW_, :], rt[:, U_, :], ACT.Ln, bias=1.0).then_inc(lnw, 1)

            def silu(t, half):
                act.wait_ge(g_ps, 2 * t + half + 1)
                nc.scalar.activation(gbuf[half][:, :], ps[:, half, 0:HALF], ACT.Silu).then_inc(silu_done, 1)

            def hT_copy(t, half):
                act.wait_ge(hT_ps, 2 * t + half + 1)
                cp(hT[half][:, :, :].rearrange("p k n -> p (k n)"), ps[:, 4 + half, 0:HALF]).then_inc(hT_done, 1)

            def xT_copy(t, s):
                act.wait_ge(xT_ps, t + 1)
                cp(xT[s][:, :, :].rearrange("p c n -> p (c n)"), ps[0:DC, 7, 0:2 * P]).then_inc(xT_done, 1)

            def tile(t, s):
                silu(t, 0)
                hT_copy(t - 1, 1)
                xT_copy(t + 1, 1 - s)
                silu(t, 1)
                hT_copy(t, 0)

            xT_copy(0, 0)
            silu(0, 0)
            xT_copy(1, 1)
            silu(0, 1)
            hT_copy(0, 0)
            with act.Fori(0, (TILES - 1) // 2) as i:
                tile(2 * i + 1, 1)
                tile(2 * i + 2, 0)
            hT_copy(TILES - 1, 1)

        @block.gpsimd
        def _(pool):
            pool.wait_ge(const_in, 80)

            def rstd_of(n, s, mv, at, done, count):
                pool.wait_ge(mv, n + 1)
                pool.tensor_tensor(st[s][:, at:at + 1], st[s][:, at - 1:at], cst[0:N, C_POW + 2:C_POW + 3], ALU.add).then_inc(veps, 1)
                pool.wait_ge(veps, count)
                pool.tensor_tensor(st[s][:, at + 1:at + 2], st[s][:, at:at + 1], cst[0:N, C_POW:C_POW + 1],
                                   ALU.pow).then_inc(done, 1)

            def pair(n, s, after):
                if after:
                    rstd_of(n + 1, 1 - s, mv1, 8, rstd1, 2 * n + 2)
                rstd_of(n, s, mv2, 12, rstd2, 2 * n + 3 if after else 2 * n + 2)
                pool.wait_ge(x2_done, n + 1)
                pool.tensor_copy(rows[:, bass.ds(n, 1), 0:D], x2[s][:, :].unsqueeze(1)).then_inc(row_done, 1)

            rstd_of(0, 0, mv1, 8, rstd1, 1)
            pair(0, 0, True)
            pair(1, 1, True)
            with pool.Fori(1, B // 2 - 1) as i:
                pair(2 * i, 0, True)
                pair(2 * i + 1, 1, True)
            pair(B - 2, 0, True)
            pair(B - 1, 1, False)

            pool.wait_ge(softp, 1)
            pool.tensor_tensor(rt[:, SC_, :], rt[:, SP_, :],
                               cst[0:N, C_POW + 1:C_POW + 2].broadcast_to([N, B * E]), ALU.pow).then_inc(root, 1)

            pool.wait_ge(slots, 1)
            pool.wait_ge(w1_set, 1)
            pool.wait_ge(fill_out, 48)
            for n in range(B):
                pool.indirect_dma_start(xs[:, :], bass.IndirectOffsetOnAxis(slot1[:, n:n + 1], 0),
                                        rows[:, n, :], None).then_inc(scat1, 16)
            pool.wait_ge(w2_set, 1)
            for n in range(B):
                pool.indirect_dma_start(xs[:, :], bass.IndirectOffsetOnAxis(slot2[:, n:n + 1], 0),
                                        rows[:, n, :], None).then_inc(scat2, 16)

            def add_rows(t, s):
                pool.wait_ge(meta_done, t + 1)
                pool.tensor_copy(idx[s][:, :], meta[:, bass.ds(t, 1), 0]).then_inc(idx_done, 1)
                pool.wait_ge(idx_done, t + 1)
                pool.wait_ge(y_done, t + 1)
                if not (isinstance(t, int) and t == 0):
                    pool.wait_ge(y_out, 16 * t)
                pool.nop(nofuse=True)
                pool.indirect_dma_start(acc[:, :], bass.IndirectOffsetOnAxis(idx[s][:, 0:1], 0),
                                        yout[s][:, :], None, compute_op=ALU.add).then_inc(y_out, 16)

            pool.wait_ge(h2_out[0], 8 * B)
            pool.wait_ge(h2_out[1], 8 * B)
            add_rows(0, 0)
            with pool.Fori(0, (TILES - 1) // 2) as i:
                add_rows(2 * i + 1, 1)
                add_rows(2 * i + 2, 0)

        @block.vector
        def _(dve):
            V = nc.vector

            def norm1(n, s, times):
                dve.wait_ge(E_ps, n + 1)
                dve.wait_ge(txt_in[s], times)
                V.tensor_tensor(h[s][0:NEMB, :], bank(s, 0)[0:NEMB, 0:D], base[:, :], ALU.add).then_inc(h_sum, 1)
                dve.wait_ge(h_sum, n + 1)
                V.bn_stats(st[s][:, 0:6], h[s][:, :]).then_inc(bn1, 1)
                dve.wait_ge(bn1, n + 1)
                dve.nop(nofuse=True)
                V.bn_aggr(st[s][:, 6:8], st[s][:, 0:6]).then_inc(mv1, 1)

            def norm1_end(n, s):
                dve.wait_ge(rstd1, n + 1)
                V.tensor_scalar(xn[s][:, :], h[s][:, :], st[s][:, 6:7], st[s][:, 9:10], ALU.subtract, ALU.mult)\
                    .then_inc(xn_done, 1)

            def gate_max(n, s):
                dve.wait_ge(lora_ps, n + 1)
                V.tensor_reduce(st[s][:, 16:17], bank(s, 2)[0:N, E * R:NLG], AX.X, ALU.max, negate=True)\
                    .then_inc(gmax, 1)

            def gated(n, s):
                dve.wait_ge(gexp, n + 1)
                V.reciprocal(st[s][:, 18:19], st[s][:, 17:18]).then_inc(grcp, 1)
                dve.wait_ge(grcp, n + 1)
                V.scalar_tensor_tensor(hg[s][:, 0:E * R].rearrange("p (e r) -> p e r", r=R),
                                       bank(s, 2)[0:N, 0:E * R].rearrange("p (e r) -> p e r", r=R), st[s][:, 18:19],
                                       hg[s][:, E * R:E * R + E].unsqueeze(2).broadcast_to([N, E, R]),
                                       ALU.mult, ALU.mult).then_inc(hg_done, 1)

            def softmax(n, s):
                dve.wait_ge(s_ps, n + 1)
                sv = ps[0:N, 4 * s:4 * s + 4, 0:NG * N].rearrange("p j (g k) -> p j g k", g=NG)
                mx = smx[s][:, 0:H].rearrange("p (j g) -> p j g", j=NJ)
                V.tensor_reduce(mx, sv, AX.X, ALU.max).then_inc(smax, 1)
                dve.wait_ge(smax, n + 1)
                V.tensor_tensor(prob[s].rearrange("p (j g k) -> p j g k", j=NJ, g=NG), sv,
                                mx.unsqueeze(3).broadcast_to([N, NJ, NG, N]), ALU.subtract).then_inc(ssub, 1)

            def attend_end(n, s):
                dve.wait_ge(pv_ps, n + 1)
                ov = bank(s, 3)[0:N, 0:H * VW].rearrange("p (h d) -> p h d", d=VW)
                V.reciprocal(smx[s][:, H:2 * H], ov[:, :, HD]).then_inc(ssum, 1)
                dve.wait_ge(ssum, n + 1)
                V.tensor_tensor(o[s][:, :].rearrange("p (h d) -> p h d", d=HD), ov[:, :, 0:HD],
                                smx[s][:, H:2 * H].unsqueeze(2).broadcast_to([N, H, HD]), ALU.mult).then_inc(o_done, 1)

            def norm2(n, s):
                dve.wait_ge(proj_ps, n + 1)
                V.tensor_tensor(h[s][:, :], bank(s, 1)[0:N, 0:D], h[s][:, :], ALU.add).then_inc(h2_done, 1)
                dve.wait_ge(h2_done, n + 1)
                V.bn_stats(st[s][:, 0:6], h[s][:, :]).then_inc(bn2, 1)
                dve.wait_ge(bn2, n + 1)
                dve.nop(nofuse=True)
                V.bn_aggr(st[s][:, 10:12], st[s][:, 0:6]).then_inc(mv2, 1)
                dve.wait_ge(rstd2, n + 1)
                V.tensor_scalar(x2[s][:, :], h[s][:, :], st[s][:, 10:11], st[s][:, 13:14], ALU.subtract, ALU.mult)\
                    .then_inc(x2_done, 1)

            def logit_copy(n, s):
                dve.wait_ge(logit_ps, n + 1)
                V.tensor_copy(logit[:, bass.ds(n, 1), :], bank(s, 3)[0:N, 0:E].unsqueeze(1)).then_inc(logit_done, 1)

            def pair(n, s, before, after, times):
                z = 1 - s
                softmax(n, s)
                if before:
                    logit_copy(n - 1, z)
                if after:
                    norm1(n + 1, z, times)
                    norm1_end(n + 1, z)
                    gate_max(n + 1, z)
                    gated(n + 1, z)
                attend_end(n, s)
                norm2(n, s)

            V.memset(filler[:, 0:D], 0.0).then_inc(fill_done, 1)
            V.memset(filler[:, WT:WT + 1], 0.0).then_inc(fill_done, 1)
            for s in range(2):
                V.memset(xnT[s][DC:DC + 1, 1, :], 1.0).then_inc(ones_done, 1)
                V.memset(oT[s][DC:DC + 1, 1, :], 1.0).then_inc(ones_done, 1)
                V.memset(va[s][:, :, HD:VW], 1.0).then_inc(ones_done, 1)
            V.memset(rows[:, :, WT:WT + 1], 1.0).then_inc(ones_done, 1)
            dve.wait_ge(const_in, 80)
            V.tensor_copy(filler[:, ID:ID + 1], cst[:, C_FILL:C_FILL + 1]).then_inc(fill_done, 1)
            V.tensor_copy(rows[:, :, ID], cst[0:N, C_TOK:C_TOK + B]).then_inc(ones_done, 1)
            dve.wait_ge(base_ps, 1)
            V.tensor_tensor(base[:, :], bank(1, 3)[0:NEMB, 0:D], base[:, :], ALU.add).then_inc(base_done, 1)
            V.memset(etab[:, 0:SH_TILES], 0)
            dve.wait_ge(base_done, 1)
            norm1(0, 0, 16)
            norm1_end(0, 0)
            gate_max(0, 0)
            gated(0, 0)
            pair(0, 0, False, True, 16)
            pair(1, 1, True, True, 32)
            with dve.Fori(1, B // 2 - 1) as i:
                pair(2 * i, 0, True, True, 16 * i + 16)
                pair(2 * i + 1, 1, True, True, 16 * i + 32)
            pair(B - 2, 0, True, True, 8 * B)
            pair(B - 1, 1, True, False, None)
            logit_copy(B - 1, 1)

            steps = [0]

            def link(ins):
                steps[0] += 1
                ins.then_inc(rstep, 1)
                dve.wait_ge(rstep, steps[0])

            def rv(k):
                return rt[:, k, :].rearrange("p (n e) -> p n e", e=E)

            def over_e(a):
                return a.unsqueeze(2).broadcast_to([N, B, E])

            def TT(out, a, b, op):
                link(V.tensor_tensor(out, a, b, op))

            def TS(out, a, c1, c2, op1, op2=None):
                link(V.tensor_scalar(out, a, c1, c2, op1, op2) if op2 is not None else V.tensor_scalar(out, a, c1, None, op1))

            dve.wait_ge(logit_done, B)
            lg = logit[:, :, :].rearrange("p n e -> p (n e)")
            V.scalar_tensor_tensor(rt[:, ABS_, :], lg, -1.0, lg, ALU.mult, ALU.max).then_inc(absl, 1)
            dve.wait_ge(uexp, 1)
            TS(rt[:, D_, :], rt[:, U_, :], 1.0, -1.0, ALU.add, ALU.add)
            TS(rt[:, A_, :], rt[:, D_, :], 1e-30, None, ALU.max)
            link(V.reciprocal(rt[:, A_, :], rt[:, A_, :]))
            TT(rt[:, A_, :], rt[:, A_, :], rt[:, U_, :], ALU.mult)
            dve.wait_ge(lnw, 1)
            TT(rt[:, A_, :], rt[:, A_, :], rt[:, LNW_, :], ALU.mult)
            link(V.scalar_tensor_tensor(rt[:, D_, :], rt[:, D_, :], 0.0, rt[:, U_, :], ALU.is_equal, ALU.mult))
            TT(rt[:, A_, :], rt[:, A_, :], rt[:, D_, :], ALU.add)
            V.scalar_tensor_tensor(rt[:, SP_, :], lg, 0.0, rt[:, A_, :], ALU.max, ALU.add).then_inc(softp, 1)
            dve.wait_ge(root, 1)
            TT(rv(A_), rv(SC_), cst[0:N, C_BIAS:C_BIAS + E].unsqueeze(1).broadcast_to([N, B, E]), ALU.add)
            iota = cst[0:N, C_IOTA:C_IOTA + B * E]
            for mask in (M1_, M2_):
                link(V.tensor_reduce(rs[:, 0, :], rv(A_), AX.X, ALU.max))
                TT(rv(mask), rv(A_), over_e(rs[:, 0, :]), ALU.is_ge)
                TT(rt[:, mask, :], rt[:, mask, :], iota, ALU.mult)
                link(V.tensor_reduce(rs[:, 1, :], rv(mask), AX.X, ALU.min))
                TT(rv(mask), iota.rearrange("p (n e) -> p n e", e=E), over_e(rs[:, 1, :]), ALU.is_equal)
                if mask == M1_:
                    link(V.scalar_tensor_tensor(rt[:, A_, :], rt[:, mask, :], -3.0e38, rt[:, A_, :], ALU.mult, ALU.add))
            V.tensor_tensor(rt[:, PICK, :], rt[:, M1_, :], rt[:, M2_, :], ALU.add).then_inc(picks, 1)
            for k, mask in enumerate((M1_, M2_)):
                TT(rt[:, D_, :], rt[:, mask, :], rt[:, SC_, :], ALU.mult)
                link(V.tensor_reduce(rs[:, 2 + k, :], rv(D_), AX.X, ALU.add))
            TT(rs[:, 4, :], rs[:, 2, :], rs[:, 3, :], ALU.add)
            TS(rs[:, 4, :], rs[:, 4, :], 1e-6, None, ALU.max)
            link(V.reciprocal(rs[:, 4, :], rs[:, 4, :]))
            for k in range(2):
                TT(rs[:, 2 + k, :], rs[:, 2 + k, :], rs[:, 4, :], ALU.mult)
            dve.wait_ge(rank_ps, 1)
            link(V.tensor_copy(rt[:, RANK, :], bank(0, 0)[0:N, 0:B * E]))
            V.tensor_copy(rt[:, CNT, :], bank(0, 1)[0:N, 0:B * E]).then_inc(rank_copied, 1)
            dve.wait_ge(rank_copied, 1)
            TT(rt[:, RANK, :], rt[:, RANK, :], rt[:, CNT, :], ALU.subtract)
            a, b = CNT, P1_
            for sh in (1, 2, 4, 8):
                w = sh * E
                link(V.tensor_copy(rt[:, b, 0:w], rt[:, a, 0:w]))
                TT(rt[:, b, w:], rt[:, a, w:], rt[:, a, 0:B * E - w], ALU.add)
                a, b = b, (P2_ if b == P1_ else P1_)
            TT(rt[:, RANK, :], rt[:, RANK, :], rt[:, a, :], ALU.add)
            count = rt[:, a, (B - 1) * E:B * E]
            TT(jcmp[:, :].rearrange("p (e j) -> p e j", e=E), count.unsqueeze(2).broadcast_to([N, E, SH_TILES]),
               cst[0:N, C_J:C_J + E * SH_TILES].rearrange("p (e j) -> p e j", e=E), ALU.is_gt)
            link(V.tensor_reduce(off[:, 0, :], jcmp[:, :].rearrange("p (e j) -> p e j", e=E), AX.X, ALU.add))
            for k, sh in enumerate((1, 2, 4)):
                link(V.tensor_copy(off[:, k + 1, 0:sh], off[:, k, 0:sh]))
                TT(off[:, k + 1, sh:], off[:, k, sh:], off[:, k, 0:E - sh], ALU.add)
            TT(off[:, 4, :], off[:, 3, :], off[:, 0, :], ALU.subtract)
            TS(off[:, 5, :], off[:, 4, :], float(P), float(SH_TILES * P), ALU.mult, ALU.add)
            TT(rv(RANK), rv(RANK), off[:, 5, :].unsqueeze(1).broadcast_to([N, B, E]), ALU.add)
            for k, (mask, slot) in enumerate(((M1_, slot1), (M2_, slot2))):
                TT(rt[:, D_, :], rt[:, mask, :], rt[:, RANK, :], ALU.mult)
                link(V.tensor_reduce(rs[:, 5 + k, :], rv(D_), AX.X, ALU.add))
                link(V.tensor_copy(slot[:, :], rs[:, 5 + k, :]))
            nt = XT_TILES - SH_TILES
            ecmp = rt[:, 0:3, :].rearrange("p a b -> p (a b)")[:, 0:nt * E]
            TT(ecmp.rearrange("p (t e) -> p t e", e=E), cst[0:N, C_T:C_T + nt * E].rearrange("p (t e) -> p t e", e=E),
               off[:, 3, :].unsqueeze(1).broadcast_to([N, nt, E]), ALU.is_ge)
            link(V.tensor_reduce(jcmp[:, 0:nt], ecmp.rearrange("p (t e) -> p t e", e=E), AX.X, ALU.add))
            TS(jcmp[:, 0:nt], jcmp[:, 0:nt], float(E - 1), 1.0, ALU.min, ALU.add)
            V.tensor_copy(etab[:, SH_TILES:], jcmp[:, 0:nt]).then_inc(slots, 1)
            dve.wait_ge(x2_out, 16 * B)
            V.tensor_copy(rows[:, :, WT], rs[:, 2, :]).then_inc(w1_set, 1)

            def hidden(t, half):
                dve.wait_ge(u_ps, 2 * t + half + 1)
                V.tensor_scalar(ubuf[half][:, :], ps[:, 2 + half, 0:HALF], -LIMIT, LIMIT, ALU.max, ALU.min)\
                    .then_inc(clip_done, 1)
                dve.wait_ge(clip_done, 2 * t + half + 1)
                dve.wait_ge(silu_done, 2 * t + half + 1)
                V.scalar_tensor_tensor(hbuf[half][:, :], gbuf[half][:, :], SILU_LIMIT, ubuf[half][:, :],
                                       ALU.min, ALU.mult).then_inc(hh_done, 1)

            def meta_copy(t, s, times):
                dve.wait_ge(x_in[s], times)
                V.tensor_copy(meta[:, bass.ds(t, 1), :], xin[s][:, ID:ROW].unsqueeze(1)).then_inc(meta_done, 1)

            def result(t, s):
                dve.wait_ge(y_ps, t + 1)
                if not (isinstance(t, int) and t < 2):
                    dve.wait_ge(y_out, 16 * t - 16)
                V.tensor_scalar(yout[s][:, :], ps[:, 6, 0:D], meta[:, bass.ds(t, 1), 1], None, ALU.mult)\
                    .then_inc(y_done, 1)

            meta_copy(0, 0, 16)
            hidden(0, 0)
            meta_copy(1, 1, 16)
            hidden(0, 1)
            dve.wait_ge(scat1, 16 * B)
            V.tensor_copy(rows[:, :, WT], rs[:, 3, :]).then_inc(w2_set, 1)

            def tile(t, s, times):
                hidden(t, 0)
                meta_copy(t + 1, 1 - s, times)
                result(t - 1, 1 - s)
                hidden(t, 1)

            tile(1, 1, 32)
            tile(2, 0, 32)
            with dve.Fori(1, (TILES - 1) // 2) as i:
                tile(2 * i + 1, 1, 16 * i + 32)
                tile(2 * i + 2, 0, 16 * i + 32)
            result(TILES - 1, 0)


ABS_, U_, LNW_, D_, A_, SP_, SC_, M1_, M2_, PICK, RANK, CNT, P1_, P2_ = range(14)


def kernel(**inputs):
    import numpy as np
    import concourse.bacc as bacc
    from concourse import mybir as _mybir
    from concourse.bass_utils import run_bass_kernel_spmd as run

    a = {k: np.asarray(v) for k, v in inputs.items()}
    f32 = np.float32

    x = a["x"].reshape(B, 3, 6, 16, 6, 16).transpose(1, 3, 5, 0, 2, 4).reshape(KP, B, NPATCH)
    patches = np.zeros((KP, B, NEMB), f32)
    patches[:, :, 1:] = x
    patches = np.ascontiguousarray(patches.reshape(6, P, B, NEMB).transpose(2, 1, 0, 3))
    proj_w = np.ascontiguousarray(a["L0_tok_proj_w"].T.reshape(6, P, D).transpose(1, 0, 2))
    mask2 = np.zeros((2, NEMB), f32)
    mask2[0, 0] = 1
    mask2[1, 1:] = 1
    cls_b = np.stack([a["L0_tok_cls_token"].reshape(D), a["L0_tok_proj_b"]])

    def heads_apart(m):
        out = np.zeros((m.shape[0], LOFF), f32)
        for part in range(2):
            to = out[:, part * QG:(part + 1) * QG].reshape(-1, NG, NJ, 32)
            to[:, :, :, 0:HD] = m[:, part * D:(part + 1) * D].reshape(-1, NG, NJ, HD)
        out[:, VOFF:] = m[:, 2 * D:]
        return out

    wa = np.zeros((DC + 1, 2, NWA), f32)
    qkv = heads_apart(a["L0_attn_qkv_w"].T)
    down = a["L0_attn_lora_a"].transpose(1, 0, 2).reshape(D, E * R)
    for c in range(2):
        wa[0:DC, c, 0:LOFF] = qkv[c * DC:(c + 1) * DC]
        wa[0:DC, c, LOFF:LOFF + E * R] = down[c * DC:(c + 1) * DC]
        wa[0:DC, c, LOFF + E * R:] = a["L0_attn_gate_w"].T[c * DC:(c + 1) * DC]
    wa[DC, 1, 0:LOFF] = heads_apart(a["L0_attn_qkv_b"][None])[0]
    lora_b = heads_apart(a["L0_attn_lora_b"].reshape(E * R, 3 * D))
    out_w = np.zeros((DC + 1, 2, D), f32)
    for c in range(2):
        out_w[0:DC, c] = a["L0_attn_proj_w"].T[c * DC:(c + 1) * DC]
    out_w[DC, 1] = a["L0_attn_proj_b"]
    gate_w = np.ascontiguousarray(a["L0_ffn_gate_w"].reshape(2, DC, E).transpose(1, 0, 2))

    p = np.arange(P)
    consts = np.zeros((P, C_ALL), f32)
    consts[:, C_ID:C_ID + P] = np.eye(P)
    consts[:, C_TRI:C_TRI + N] = p[:, None] < np.arange(N)[None, :]
    consts[:, C_ONE:C_ONE + N] = 1
    consts[:, C_IOTA:C_IOTA + B * E] = np.tile(np.arange(E) - E, B)
    consts[:, C_J:C_J + E * SH_TILES] = np.tile(P * np.arange(SH_TILES), E)
    consts[:, C_T:C_T + (RT_TILES + 1) * E] = np.repeat(np.arange(RT_TILES + 1), E)
    consts[:, C_POW] = -0.5
    consts[:, C_POW + 1] = 0.5
    consts[:, C_POW + 2] = EPS
    consts[:, C_TOK:C_TOK + B] = N * np.arange(B)[None, :] + p[:, None]
    consts[:, C_FILL] = T + p
    consts[:, C_BIAS:C_BIAS + E] = a["L0_ffn_gate_bias"][None, :]

    nc = bacc.Bacc("TRN2", target_bir_lowering=False, num_devices=1)
    arrays = {
        "patches": patches, "txt": a["txt"], "proj_w": proj_w, "mask2": mask2, "cls_b": cls_b,
        "pos": a["L0_tok_pos_embedding"].reshape(NEMB, D), "wa": wa, "lora_b": lora_b, "out_w": out_w,
        "gate_w": gate_w, "consts": consts, "w1": a["L0_ffn_w1"], "w2": a["L0_ffn_w2"], "w3": a["L0_ffn_w3"],
        "w1s": a["L0_ffn_w1s"], "w2s": a["L0_ffn_w2s"], "w3s": a["L0_ffn_w3s"],
    }
    arrays = {f"in_{k}": np.ascontiguousarray(v) for k, v in arrays.items()}
    args = [nc.dram_tensor(k, v.shape, _mybir.dt.from_np(v.dtype), kind="ExternalInput").ap() for k, v in arrays.items()]
    args.append(nc.dram_tensor("acc", (T + P, D), F32, kind="ExternalOutput").ap())
    args.append(nc.dram_tensor("xs", (XT_TILES * P, ROW), F32, kind="Internal").ap())
    program(nc, *args)
    r = run(nc, [arrays], core_ids=[0])
    return r.results[0]["acc"][0:T].reshape(B, N, D)
```

```python
from contextlib import ExitStack

import concourse.bass as bass
from concourse import mybir

F32 = mybir.dt.float32
U32 = mybir.dt.uint32
I32 = mybir.dt.int32
ALU = mybir.AluOpType
ACT = mybir.ActivationFunctionType
AX = mybir.AxisListType

B, NPATCH, NTXT, D = 16, 36, 77, 192
NEMB = NPATCH + 1
N = NEMB + NTXT
T = B * N
KP = 768
H, HD, NG, NJ = 12, 16, 3, 4
E, R, I = 8, 8, 768
DC = D // 2
LIMIT = 10.0
SILU_LIMIT = 9.999546021312976
EPS = 1e-5
SCALE = HD ** -0.5
QG = NG * 128
QOFF, KOFF, VOFF, LOFF = 0, QG, 2 * QG, 2 * QG + D
NLG = E * R + E
NWA = LOFF + NLG
VW = HD + 1

P = 128
PP = D - P
MOST = -(-T // P)
REGION = (MOST + 1) * P
TILES = (2 * T + E * (P - 1)) // P
SPARE = TILES + 1 - -(-2 * T // P)
LOADS = TILES + 1
ROW = D + 2
ID, WT = D, D + 1
HALF = I // 2
KH = HALF // P
LATE = 4
ET = -(-B * NPATCH // P)
GB = 2
GE = GB * E

C_ID, C_TRI, C_ONE, C_IOTA = 0, P, P + N, 2 * P + N
C_J = C_IOTA + GE
C_T = C_J + E * MOST
C_TT = C_T + LOADS * E
C_POW = C_TT + LOADS
C_TOK = C_POW + 3
C_FILL = C_TOK + B
C_REG = C_FILL + 1
C_BIAS = C_REG + E
C_ALL = C_BIAS + GE


def program(nc, patches, txt, proj_w, pos_rows, small, wa, bqk, bv, out_w, gate_w, consts, w1, w2, w3, w1s, w2s, w3s,
            acc, xs, emb):
    with ExitStack() as ctx:
        def sb(name, shape, dt=F32):
            return ctx.enter_context(nc.sbuf_tensor(name, shape, dt))

        def sem(name):
            return ctx.enter_context(nc.semaphore(name))

        w13 = sb("w13", [P, E + 1, 2 * 2 * I])
        wdn = sb("wdn", [P, E + 1, (I // P) * D])
        late13 = w13[:, E + 1 - LATE:, :].rearrange("p a b -> p (a b)")
        late2 = wdn[:, E + 1 - LATE:, :].rearrange("p a b -> p (a b)")
        used = [0, 0]

        def lend(k, rows_, size):
            part = (late13, late2)[k][0:rows_, used[k]:used[k] + size]
            used[k] += size
            assert used[k] <= LATE * (4 * I, (I // P) * D)[k]
            return part

        prob = [lend(0, N, H * N) for _ in range(2)]
        probT = [lend(0, N, H * N) for _ in range(2)]
        qT = [lend(0, P, NG * N) for _ in range(2)]
        kT = [lend(0, P, NG * N) for _ in range(2)]
        patch_sb = lend(0, P, 6 * B * NPATCH).rearrange("p (k m) -> p k m", k=6)
        wa_sb = lend(1, P, 2 * NWA).rearrange("p (c n) -> p c n", c=2)
        pw_sb = lend(1, P, 6 * D).rearrange("p (k d) -> p k d", k=6)
        pr_sb = lend(1, P, ET * D).rearrange("p (k d) -> p k d", k=ET)

        cst = sb("cst", [P, C_ALL])
        small_sb = sb("small_sb", [1, 3 * D])
        ow_sb = sb("ow_sb", [DC + 1, 2, D])
        bqk_sb = sb("bqk_sb", [P, 2 * NG])
        bv_sb = sb("bv_sb", [N, D])
        gw_sb = sb("gw_sb", [DC, 2, E])
        rows = sb("rows", [N, B, ROW])
        row1 = [sb(f"row1_{s}", [N, ROW]) for s in range(2)]
        row2 = [sb(f"row2_{s}", [N, ROW]) for s in range(2)]
        filler = sb("filler", [P, ROW])
        x2 = [sb(f"x2{s}", [N, D]) for s in range(2)]
        h = [sb(f"h{s}", [N, D]) for s in range(2)]
        h2 = [sb(f"h2{s}", [N, D]) for s in range(2)]
        xh = [sb(f"xh{s}", [N, 2 * P]) for s in range(2)]
        xT1 = [lend(0, P, 2 * N).rearrange("p (c n) -> p c n", c=2) for _ in range(2)]
        st = [sb(f"st{s}", [N, 32]) for s in range(2)]
        va = [sb(f"va{s}", [N, H, VW]) for s in range(2)]
        smx = [sb(f"smx{s}", [N, 2 * H]) for s in range(2)]
        o = [sb(f"o{s}", [N, D]) for s in range(2)]
        oT = [lend(0, DC + 1, 2 * N).rearrange("p (c n) -> p c n", c=2) for _ in range(2)]
        x2T = [sb(f"x2T{s}", [DC, 2, N]) for s in range(2)]
        rt = sb("rt", [N, 18, GE])
        rs = sb("rs", [N, 8, GB])
        run = sb("run", [N, E])
        off = sb("off", [N, 6, E])
        jcmp = sb("jcmp", [N, LOADS * E])
        tv = sb("tv", [N, 3, LOADS])
        slot1 = sb("slot1", [N, GB], U32)
        slot2 = sb("slot2", [N, GB], U32)
        etab = sb("etab", [1, LOADS + 1], I32)
        rtab = sb("rtab", [1, LOADS], I32)
        wtab = sb("wtab", [1, LOADS], I32)
        ftab = sb("ftab", [1, E], I32)

        xin = [sb(f"xin{s}", [P, ROW]) for s in range(2)]
        xT = [sb(f"xT{s}", [DC, 2, P]) for s in range(2)]
        meta = sb("meta", [P, LOADS, 2])
        gbuf = [sb(f"gbuf{i}", [P, HALF]) for i in range(2)]
        ubuf = [sb(f"ubuf{i}", [P, HALF]) for i in range(2)]
        hbuf = [sb(f"hbuf{i}", [P, HALF]) for i in range(2)]
        hT = [sb(f"hT{i}", [P, KH, P]) for i in range(2)]
        yout = [sb(f"yout{s}", [P, D]) for s in range(2)]
        idx = [sb(f"idx{s}", [P, 1], U32) for s in range(2)]
        emb_sb = lend(0, P, ET * D).rearrange("p (k d) -> p k d", k=ET)
        clsrow = small_sb[:, D:2 * D]

        ps = ctx.enter_context(nc.psum_tensor("ps", [P, 8, 512], F32))
        ident = cst[:, C_ID:C_ID + P]
        LG, U, Z, Z2, Q, SP, SC, A, AM, M1, M2, PICK, RANK, TMP, W0, W1, W2, W3 = range(18)

        def bank(b):
            return ps[:, b, :]

        const_in, wa_in, w_shared, w_in = (sem(x) for x in ("const_in", "wa_in", "w_shared", "w_in"))
        h_in = [sem(f"h_in{s}") for s in range(2)]
        emb_ps, emb_done, emb_out, cls_done, ones_done = (sem(x) for x in ("emb_ps", "emb_done", "emb_out", "cls_done", "ones_done"))
        xT_ps, lora_ps, hgT_ps, q_ps, k_ps, v_ps = (sem(x) for x in ("xT_ps", "lora_ps", "hgT_ps", "q_ps", "k_ps", "v_ps"))
        s_ps, pT_ps, pv_ps, oT_ps, proj_ps = (sem(x) for x in ("s_ps", "pT_ps", "pv_ps", "oT_ps", "proj_ps"))
        x2T_ps, logit_ps = sem("x2T_ps"), sem("logit_ps")
        bn1, mv1, veps, rstd1, xn_done, xT_done = (sem(x) for x in ("bn1", "mv1", "veps", "rstd1", "xn_done", "xT_done"))
        gmax, gexp, grcp, hg_done, hgT_done = (sem(x) for x in ("gmax", "gexp", "grcp", "hg_done", "hgT_done"))
        q_done, k_done, v_done = sem("q_done"), sem("k_done"), sem("v_done")
        smax, ssub, p_done, pT_done = (sem(x) for x in ("smax", "ssub", "p_done", "pT_done"))
        ssum, o_done, oT_done, h2_done = sem("ssum"), sem("o_done"), sem("oT_done"), sem("h2_done")
        bn2, mv2, rstd2, x2_done, x2T_done, row_done = (sem(x) for x in ("bn2", "mv2", "rstd2", "x2_done", "x2T_done", "row_done"))
        sum_done = sem("sum_done")
        acc_out = [sem(f"acc_out{s}") for s in range(2)]
        g_ps, u_ps, act_done, gs_done, clip_done, hh_done = (sem(x) for x in ("g_ps", "u_ps", "act_done", "gs_done", "clip_done", "hh_done"))
        hT_ps, hT_done, y_ps = sem("hT_ps"), sem("hT_done"), sem("y_ps")
        logit_done, absl, uexp, softp, root, picks = (sem(x) for x in ("logit_done", "absl", "uexp", "softp", "root", "picks"))
        rank_ps, rank_copied, slots, weights, rstep = (sem(x) for x in ("rank_ps", "rank_copied", "slots", "weights", "rstep"))
        copied, weighted, scat1, scat2 = sem("copied"), sem("weighted"), sem("scat1"), sem("scat2")
        tables, fill_done, fill_out, spare_out = sem("tables"), sem("fill_done"), sem("fill_out"), sem("spare_out")
        x_in = [sem(f"x_in{s}") for s in range(2)]
        rxT_ps, rxT_done, meta_done = sem("rxT_ps"), sem("rxT_done"), sem("meta_done")
        rg_ps, ru_ps, silu_done, rclip_done, rhh_done = (sem(x) for x in ("rg_ps", "ru_ps", "silu_done", "rclip_done", "rhh_done"))
        rhT_ps, rhT_done, ry_ps, y_done, idx_done, y_out = (sem(x) for x in ("rhT_ps", "rhT_done", "ry_ps", "y_done", "idx_done", "y_out"))

        block = ctx.enter_context(nc.Block())

        @block.sync
        def _(sp):
            def load_h(n, s):
                sp.dma_start(h[s][0:1, :], clsrow).then_inc(h_in[s], 16)
                sp.dma_start(h[s][1:NEMB, :], emb[bass.ds(n * NPATCH, NPATCH), :]).then_inc(h_in[s], 16)
                sp.dma_start(h[s][NEMB:N, :], txt[bass.ds(n, 1)].rearrange("a t d -> (a t) d")).then_inc(h_in[s], 16)

            sp.dma_start(cst[:, :], consts[:, :]).then_inc(const_in, 16)
            sp.dma_start(small_sb[:, :], small[:, :]).then_inc(const_in, 16)
            sp.dma_start(pw_sb, proj_w[:, :, :]).then_inc(const_in, 16)
            sp.dma_start(patch_sb, patches[:, :, :]).then_inc(const_in, 16)
            sp.dma_start(pr_sb, pos_rows[:, :, :]).then_inc(const_in, 16)
            for dst, src in ((wa_sb, wa), (gw_sb[:, :, :], gate_w), (ow_sb[:, :, :], out_w)):
                sp.dma_start(dst, src[:, :, :]).then_inc(wa_in, 16)
            sp.dma_start(bqk_sb[:, :], bqk[:, :]).then_inc(wa_in, 16)
            sp.dma_start(bv_sb[:, :], bv[:, :]).then_inc(wa_in, 16)
            sp.wait_ge(emb_done, ET)
            full = B * NPATCH // P
            sp.dma_start(emb[0:full * P, :].rearrange("(k p) d -> p k d", p=P), emb_sb[:, 0:full, :]).then_inc(emb_out, 16)
            sp.dma_start(emb[full * P:, :], emb_sb[0:B * NPATCH - full * P, full, :]).then_inc(emb_out, 16)
            sp.wait_ge(cls_done, 1)
            sp.wait_ge(emb_out, 32)
            load_h(0, 0)
            load_h(1, 1)
            sp.wait_ge(fill_done, 3)
            sp.dma_start(xs[E * REGION:, :].rearrange("(t p) c -> p t c", p=P),
                         filler[:, :].unsqueeze(1).broadcast_to([P, SPARE, ROW])).then_inc(spare_out, 16)
            sp.dma_start(acc[T:T + P, :], filler[:, 0:D]).then_inc(spare_out, 16)

            def store_sum(n, s):
                sp.wait_ge(sum_done, n + 1)
                sp.dma_start(acc[bass.ds(n * N, N), :], h2[s][:, :]).then_inc(acc_out[s], 16)

            def step(n, s, before, more):
                if before:
                    store_sum(n - 1, 1 - s)
                if more:
                    sp.wait_ge(h2_done, n + 1)
                    load_h(n + 2, s)

            step(0, 0, False, True)
            step(1, 1, True, True)
            with sp.Fori(1, B // 2 - 1) as i:
                step(2 * i, 0, True, True)
                step(2 * i + 1, 1, True, True)
            step(B - 2, 0, True, False)
            step(B - 1, 1, True, False)
            store_sum(B - 1, 1)

            sp.wait_ge(tables, 1)
            for e in range(E):
                first = sp.value_load(ftab[0:1, e:e + 1], min_val=e * REGION, max_val=e * REGION + MOST * P)
                sp.dma_start(xs[bass.ds(first, P), :], filler[:, :]).then_inc(fill_out, 16)

            def load_tile(t, s):
                row = sp.value_load(rtab[0:1, bass.ds(t, 1)], min_val=0, max_val=E * REGION + (SPARE - 1) * P)
                weights_in = sp.value_load(wtab[0:1, bass.ds(t, 1)], min_val=48 * (E - LATE), max_val=48 * E)
                sp.wait_ge(w_in, weights_in)
                sp.nop(nofuse=True)
                if not (isinstance(t, int) and t < 2):
                    sp.wait_ge(rxT_ps, t - 1)
                    sp.wait_ge(meta_done, t - 1)
                sp.nop(nofuse=True)
                sp.dma_start(xin[s][:, :], xs[bass.ds(row, P), :]).then_inc(x_in[s], 16)

            sp.wait_ge(spare_out, 32)
            sp.wait_ge(fill_out, 16 * E)
            sp.wait_ge(scat1, 16 * B)
            sp.wait_ge(scat2, 16 * B)
            sp.wait_ge(w_in, 48 * (E - LATE))
            load_tile(0, 0)
            load_tile(1, 1)
            with sp.Fori(1, LOADS // 2) as i:
                load_tile(2 * i, 0)
                load_tile(2 * i + 1, 1)
            load_tile(LOADS - 1, 0)
            sp.wait_ge(acc_out[0], 8 * B)
            sp.wait_ge(acc_out[1], 8 * B)
            sp.wait_ge(x_in[0], 8 * (LOADS + 1))
            sp.wait_ge(x_in[1], 8 * (LOADS - 1))
            sp.wait_ge(y_out, 16 * TILES)

        @block.tensor
        def _(pe):
            mm = nc.tensor.matmul

            pe.wait_ge(const_in, 80)
            for t in range(ET):
                w = min(P, B * NPATCH - t * P)
                for k in range(6):
                    mm(bank(t)[0:w, 0:D], patch_sb[:, k, t * P:t * P + w], pw_sb[:, k, :], start=(k == 0), stop=False)
                mm(bank(t)[0:w, 0:D], cst[0:1, C_ONE:C_ONE + w], small_sb[:, 0:D], start=False, stop=True)\
                    .then_inc(emb_ps, 1)

            def transpose_x(n, s):
                pe.wait_ge(xn_done, n + 1)
                nc.tensor.transpose(bank(2)[:, 0:N], xh[s][:, 0:P], ident[0:N, 0:N])
                nc.tensor.transpose(bank(2)[0:PP, N:2 * N], xh[s][:, P:D], ident[0:N, 0:N]).then_inc(xT_ps, 1)

            def lora_down(n, s):
                pe.wait_ge(xT_done, 2 * n + 2)
                out = bank(0)[0:N, 0:NLG]
                mm(out, xT1[s][:, 0, :], wa_sb[:, 0, LOFF:NWA], start=True, stop=False)
                mm(out, xT1[s][0:PP, 1, :], wa_sb[0:PP, 1, LOFF:NWA], start=False, stop=True).then_inc(lora_ps, 1)

            def transpose_hg(n, s):
                pe.wait_ge(hg_done, n + 1)
                nc.tensor.transpose(bank(2)[:, 0:N], xh[s][:, P:2 * P], ident[0:N, 0:N]).then_inc(hgT_ps, 1)

            def qkv(n, s):
                pe.wait_ge(hgT_done, n + 1)
                for off0, b, done in ((QOFF, 1, q_ps), (KOFF, 2, k_ps)):
                    for g in range(NG):
                        cols = slice(off0 + g * P, off0 + (g + 1) * P)
                        for c in range(2):
                            last = mm(bank(b)[:, g * N:(g + 1) * N], wa_sb[:, c, cols], xT1[s][:, c, :],
                                      start=(c == 0), stop=(c == 1))
                    last.then_inc(done, 1)
                if not (isinstance(n, int) and n == 0):
                    pe.wait_ge(h2_done, n)
                for c in range(2):
                    last = mm(bank(3)[0:N, 0:D], xT1[s][:, c, :], wa_sb[:, c, VOFF:LOFF], start=(c == 0), stop=(c == 1))
                last.then_inc(v_ps, 1)

            def scores(n, s):
                pe.wait_ge(q_done, n + 1)
                pe.wait_ge(k_done, n + 1)
                pe.wait_ge(v_done, n + 1)
                for j in range(NJ):
                    for g in range(NG):
                        at = slice(32 * j, 32 * j + HD)
                        last = mm(bank(j)[0:N, g * N:(g + 1) * N], qT[s][at, g * N:(g + 1) * N],
                                  kT[s][at, g * N:(g + 1) * N], start=True, stop=True)
                    if j % 2:
                        last.then_inc(s_ps, 1)

            def transpose_p(n, s, half):
                pe.wait_ge(p_done, 2 * n + half + 1)
                for a in range(6 * half, 6 * half + 6):
                    last = nc.tensor.transpose(bank(a // 3)[0:N, (a % 3) * N:(a % 3 + 1) * N],
                                               prob[s][:, a * N:(a + 1) * N], ident[0:N, 0:N])
                last.then_inc(pT_ps, 1)

            def weigh_v(n, s):
                for a in range(H):
                    if a % 6 == 0:
                        pe.wait_ge(pT_done, 2 * n + a // 6 + 1)
                    head = NJ * (a % NG) + a // NG
                    last = mm(bank(0)[0:N, head * VW:(head + 1) * VW], probT[s][:, a * N:(a + 1) * N],
                              va[s][:, head, :], start=True, stop=True)
                last.then_inc(pv_ps, 1)

            def transpose_o(n, s):
                pe.wait_ge(o_done, n + 1)
                for c in range(2):
                    last = nc.tensor.transpose(bank(1)[0:DC, c * N:(c + 1) * N], o[s][:, c * DC:(c + 1) * DC],
                                               ident[0:N, 0:N])
                last.then_inc(oT_ps, 1)

            def project(n, s):
                pe.wait_ge(oT_done, n + 1)
                out = bank(3)[0:N, 0:D]
                mm(out, oT[s][0:DC, 0, :], ow_sb[0:DC, 0, :], start=True, stop=False)
                mm(out, oT[s][0:DC + 1, 1, :], ow_sb[0:DC + 1, 1, :], start=False, stop=True).then_inc(proj_ps, 1)

            def transpose_x2(n, s):
                pe.wait_ge(x2_done, n + 1)
                for c in range(2):
                    last = nc.tensor.transpose(bank(6)[0:DC, c * N:(c + 1) * N], x2[s][:, c * DC:(c + 1) * DC],
                                               ident[0:N, 0:N])
                last.then_inc(x2T_ps, 1)

            def route(n, s):
                pe.wait_ge(x2T_done, n + 1)
                for c in range(2):
                    last = mm(bank(6)[0:N, 2 * N:2 * N + E], x2T[s][:, c, :], gw_sb[:, c, :], start=(c == 0), stop=(c == 1))
                last.then_inc(logit_ps, 1)

            def rank(g):
                pe.wait_ge(picks, g + 1)
                mm(bank(5)[0:N, 0:GE], cst[0:N, C_TRI:C_TRI + N], rt[:, PICK, :], start=True, stop=True)
                mm(bank(5)[0:N, GE:2 * GE], cst[0:N, C_ONE:C_ONE + N], rt[:, PICK, :], start=True, stop=True)\
                    .then_inc(rank_ps, 1)

            def shared_in(n, s, half, up):
                for c in range(2):
                    at = c * 2 * I + up * I + half * HALF
                    last = mm(bank(4 + up)[0:N, 0:HALF], x2T[s][:, c, :], w13[0:DC, 0, at:at + HALF],
                              start=(c == 0), stop=(c == 1))
                last.then_inc((g_ps, u_ps)[up], 1)

            def shared_turn(n, half):
                pe.wait_ge(hh_done, 2 * n + half + 1)
                if half == 0:
                    pe.wait_ge(logit_done, n + 1)
                for k in range(KH):
                    last = nc.tensor.transpose(bank(6)[:, k * N:(k + 1) * N], hbuf[half][0:N, k * P:(k + 1) * P],
                                               ident[0:N, 0:N])
                last.then_inc(hT_ps, 1)

            def shared_down(n, half):
                pe.wait_ge(hT_done, 2 * n + half + 1)
                if half == 0 and not (isinstance(n, int) and n == 0):
                    pe.wait_ge(sum_done, n)
                for k in range(KH):
                    kk = half * KH + k
                    last = mm(bank(7)[0:N, 0:D], hT[half][:, k, 0:N], wdn[:, 0, kk * D:(kk + 1) * D],
                              start=(kk == 0), stop=(kk == I // P - 1))
                if half == 1:
                    last.then_inc(y_ps, 1)

            def step(n, s, before, after, ranks, ranked):
                z = 1 - s
                if before:
                    transpose_x2(n - 1, z)
                scores(n, s)
                if before:
                    route(n - 1, z)
                    shared_in(n - 1, z, 0, 0)
                    if ranked is not None:
                        pe.wait_ge(rank_copied, ranked)
                    shared_in(n - 1, z, 0, 1)
                transpose_p(n, s, 0)
                transpose_p(n, s, 1)
                if before:
                    pe.wait_ge(act_done, 2 * n - 1)
                    pe.wait_ge(gs_done, 2 * n - 1)
                    shared_in(n - 1, z, 1, 0)
                weigh_v(n, s)
                if before:
                    shared_turn(n - 1, 0)
                    shared_in(n - 1, z, 1, 1)
                transpose_o(n, s)
                if after:
                    transpose_x(n + 1, z)
                if before:
                    shared_down(n - 1, 0)
                    shared_turn(n - 1, 1)
                project(n, s)
                if after:
                    lora_down(n + 1, z)
                if before:
                    shared_down(n - 1, 1)
                if after:
                    transpose_hg(n + 1, z)
                    qkv(n + 1, z)
                if ranks is not None:
                    rank(ranks)

            pe.wait_ge(wa_in, 80)
            pe.wait_ge(ones_done, 6)
            pe.wait_ge(emb_done, ET)
            transpose_x(0, 0)
            lora_down(0, 0)
            transpose_hg(0, 0)
            qkv(0, 0)
            step(0, 0, False, True, None, None)
            pe.wait_ge(w_shared, 48)
            step(1, 1, True, True, None, None)
            step(2, 0, True, True, None, None)
            step(3, 1, True, True, 0, None)
            with pe.Fori(2, B // 2 - 1) as i:
                step(2 * i, 0, True, True, None, i - 1)
                step(2 * i + 1, 1, True, True, i - 1, None)
            step(B - 2, 0, True, True, None, B // 2 - 2)
            step(B - 1, 1, True, False, B // 2 - 2, None)
            transpose_x2(B - 1, 1)
            route(B - 1, 1)
            shared_in(B - 1, 1, 0, 0)
            pe.wait_ge(rank_copied, B // 2 - 1)
            shared_in(B - 1, 1, 0, 1)
            pe.wait_ge(act_done, 2 * B - 1)
            pe.wait_ge(gs_done, 2 * B - 1)
            shared_in(B - 1, 1, 1, 0)
            shared_turn(B - 1, 0)
            shared_in(B - 1, 1, 1, 1)
            shared_down(B - 1, 0)
            shared_turn(B - 1, 1)
            shared_down(B - 1, 1)
            rank(B // 2 - 1)
            pe.wait_ge(rank_copied, B // 2)

            def x_transpose(t, s, times):
                pe.wait_ge(x_in[s], times)
                for c in range(2):
                    last = nc.tensor.transpose(ps[0:DC, 7, c * P:(c + 1) * P], xin[s][:, c * DC:(c + 1) * DC], ident)
                last.then_inc(rxT_ps, 1)

            def gate_up(e, s, half, up):
                for c in range(2):
                    at = c * 2 * I + up * I + half * HALF
                    last = mm(ps[:, 2 * up + half, 0:HALF], xT[s][:, c, :], w13[0:DC, e, at:at + HALF],
                              start=(c == 0), stop=(c == 1))
                last.then_inc((rg_ps, ru_ps)[up], 1)

            def h_transpose(t, half):
                pe.wait_ge(rhh_done, 2 * t + half + 1)
                for k in range(KH):
                    last = nc.tensor.transpose(ps[:, 4 + half, k * P:(k + 1) * P], hbuf[half][:, k * P:(k + 1) * P], ident)
                last.then_inc(rhT_ps, 1)

            def down(t, e, half):
                pe.wait_ge(rhT_done, 2 * t + half + 1)
                if half == 0 and not (isinstance(t, int) and t == 0):
                    pe.wait_ge(y_done, t)
                for k in range(KH):
                    kk = half * KH + k
                    last = mm(ps[:, 6, 0:D], hT[half][:, k, :], wdn[:, e, kk * D:(kk + 1) * D],
                              start=(kk == 0), stop=(kk == I // P - 1))
                if half == 1:
                    last.then_inc(ry_ps, 1)

            def tile(t, s, e, e_before, times):
                pe.wait_ge(rxT_done, t + 1)
                gate_up(e, s, 0, 0)
                h_transpose(t - 1, 1)
                gate_up(e, s, 0, 1)
                down(t - 1, e_before, 1)
                x_transpose(t + 1, 1 - s, times)
                gate_up(e, s, 1, 0)
                h_transpose(t, 0)
                gate_up(e, s, 1, 1)
                down(t, e, 0)

            def experts(t, n):
                _, e = nc.values_load_multi_w_load_instructions(
                    etab[0:1, bass.ds(t, n)], engines=(mybir.EngineType.PE,), min_val=0, max_val=E,
                    skip_runtime_bounds_check_because="the router writes 1 to E")
                return e

            x_transpose(0, 0, 16)
            e0, = experts(0, 1)
            pe.wait_ge(rxT_done, 1)
            gate_up(e0, 0, 0, 0)
            gate_up(e0, 0, 0, 1)
            x_transpose(1, 1, 16)
            gate_up(e0, 0, 1, 0)
            h_transpose(0, 0)
            gate_up(e0, 0, 1, 1)
            down(0, e0, 0)
            with pe.Fori(0, (TILES - 1) // 2) as i:
                ea, eb, ec = experts(2 * i, 3)
                tile(2 * i + 1, 1, eb, ea, 16 * i + 32)
                tile(2 * i + 2, 0, ec, eb, 16 * i + 32)
            ea, eb = experts(TILES - 2, 2)
            tile(TILES - 1, 1, eb, ea, 8 * (LOADS + 1))
            h_transpose(TILES - 1, 1)
            down(TILES - 1, eb, 1)

        @block.scalar
        def _(act):
            cp = nc.scalar.copy
            act.wait_ge(const_in, 80)
            act.wait_ge(wa_in, 80)
            for src, at in ((w1s, 0), (w3s, I)):
                act.dma_start(w13[0:DC, 0, :].rearrange("p (c m) -> p c m", c=2)[:, :, at:at + I],
                              src.rearrange("(c p) i -> p c i", c=2)).then_inc(w_shared, 16)
            act.dma_start(wdn[:, 0, :].rearrange("p (k d) -> p k d", d=D),
                          w2s.rearrange("(k p) d -> p k d", p=P)).then_inc(w_shared, 16)

            def load_expert(e):
                for src, at in ((w1, 0), (w3, I)):
                    act.dma_start(w13[0:DC, bass.ds(e + 1, 1), :].rearrange("p a (c m) -> p (a c) m", c=2)[:, :, at:at + I],
                                  src[bass.ds(e, 1)].rearrange("a (c p) i -> p (a c) i", c=2)).then_inc(w_in, 16)
                act.dma_start(wdn[:, bass.ds(e + 1, 1), :].rearrange("p a (k d) -> p (a k) d", d=D),
                              w2[bass.ds(e, 1)].rearrange("a (k p) d -> p (a k) d", p=P)).then_inc(w_in, 16)

            def x_copies(n, s):
                act.wait_ge(xT_ps, n + 1)
                cp(xT1[s][:, 0, :], bank(2)[:, 0:N]).then_inc(xT_done, 1)
                cp(xT1[s][0:PP, 1, :], bank(2)[0:PP, N:2 * N]).then_inc(xT_done, 1)

            def gate_exp(n, s):
                act.wait_ge(gmax, n + 1)
                nc.scalar.activation(st[s][:, 20:20 + E], bank(0)[0:N, E * R:NLG], ACT.Exp,
                                     bias=st[s][:, 16:17], accum_out=st[s][:, 17:18]).then_inc(gexp, 1)

            def hg_copy(n, s):
                act.wait_ge(hgT_ps, n + 1)
                cp(xT1[s][:, 1, :], bank(2)[:, 0:N]).then_inc(hgT_done, 1)

            def p_exp(n, s, half):
                act.wait_ge(ssub, 2 * n + half + 1)
                part = prob[s][:, half * 6 * N:(half + 1) * 6 * N]
                nc.scalar.activation(part, part, ACT.Exp, scale=SCALE).then_inc(p_done, 1)

            def pT_copy(n, s, half):
                act.wait_ge(pT_ps, 2 * n + half + 1)
                cp(probT[s][:, half * 6 * N:(half + 1) * 6 * N].rearrange("p (b m) -> p b m", b=2),
                   ps[0:N, 2 * half:2 * half + 2, 0:3 * N]).then_inc(pT_done, 1)

            def oT_copy(n, s):
                act.wait_ge(oT_ps, n + 1)
                cp(oT[s][0:DC, :, :].rearrange("p c n -> p (c n)"), bank(1)[0:DC, 0:2 * N]).then_inc(oT_done, 1)

            def x2T_copy(n, s):
                act.wait_ge(x2T_ps, n + 1)
                cp(x2T[s][:, :, :].rearrange("p c n -> p (c n)"), bank(6)[0:DC, 0:2 * N]).then_inc(x2T_done, 1)

            def shared_tanh(n, half):
                act.wait_ge(g_ps, 2 * n + half + 1)
                nc.scalar.activation(gbuf[half][0:N, :], bank(4)[0:N, 0:HALF], ACT.Tanh, scale=0.5).then_inc(act_done, 1)

            def shared_turned(n, half):
                act.wait_ge(hT_ps, 2 * n + half + 1)
                nc.scalar.activation(hT[half][:, :, 0:N], bank(6)[:, 0:KH * N].rearrange("p (k n) -> p k n", k=KH),
                                     ACT.Copy, scale=0.5).then_inc(hT_done, 1)

            def group_exp(g):
                act.wait_ge(absl, g + 1)
                nc.scalar.activation(rt[:, U, :], rt[:, TMP, :], ACT.Exp, scale=-1.0).then_inc(uexp, 1)

            def step(n, s, before, after, group):
                z = 1 - s
                if before:
                    x2T_copy(n - 1, z)
                p_exp(n, s, 0)
                if before:
                    shared_tanh(n - 1, 0)
                p_exp(n, s, 1)
                if group is not None:
                    group_exp(group)
                pT_copy(n, s, 0)
                pT_copy(n, s, 1)
                if before:
                    shared_tanh(n - 1, 1)
                    shared_turned(n - 1, 0)
                oT_copy(n, s)
                if after:
                    x_copies(n + 1, z)
                if before:
                    shared_turned(n - 1, 1)
                if after:
                    gate_exp(n + 1, z)
                    hg_copy(n + 1, z)

            x_copies(0, 0)
            gate_exp(0, 0)
            hg_copy(0, 0)
            with act.Fori(0, E - LATE) as e:
                load_expert(e)
            step(0, 0, False, True, None)
            step(1, 1, True, True, None)
            step(2, 0, True, True, 0)
            step(3, 1, True, True, None)
            with act.Fori(2, B // 2 - 1) as i:
                step(2 * i, 0, True, True, i - 1)
                step(2 * i + 1, 1, True, True, None)
            step(B - 2, 0, True, True, B // 2 - 2)
            step(B - 1, 1, True, False, None)
            act.wait_ge(proj_ps, B)
            act.wait_ge(emb_out, 32)
            act.wait_ge(w_in, 48 * (E - LATE))
            with act.Fori(E - LATE, E) as e:
                load_expert(e)
            x2T_copy(B - 1, 1)
            shared_tanh(B - 1, 0)
            group_exp(B // 2 - 1)
            shared_tanh(B - 1, 1)
            shared_turned(B - 1, 0)
            shared_turned(B - 1, 1)

            def silu(t, half):
                act.wait_ge(rg_ps, 2 * t + half + 1)
                nc.scalar.activation(gbuf[half][:, :], ps[:, half, 0:HALF], ACT.Silu).then_inc(silu_done, 1)

            def hT_copy(t, half):
                act.wait_ge(rhT_ps, 2 * t + half + 1)
                cp(hT[half][:, :, :].rearrange("p k n -> p (k n)"), ps[:, 4 + half, 0:HALF]).then_inc(rhT_done, 1)

            def xT_copy(t, s):
                act.wait_ge(rxT_ps, t + 1)
                cp(xT[s][:, :, :].rearrange("p c n -> p (c n)"), ps[0:DC, 7, 0:2 * P]).then_inc(rxT_done, 1)

            def tile(t, s):
                silu(t, 0)
                hT_copy(t - 1, 1)
                xT_copy(t + 1, 1 - s)
                silu(t, 1)
                hT_copy(t, 0)

            xT_copy(0, 0)
            silu(0, 0)
            xT_copy(1, 1)
            silu(0, 1)
            hT_copy(0, 0)
            with act.Fori(0, (TILES - 1) // 2) as i:
                tile(2 * i + 1, 1)
                tile(2 * i + 2, 0)
            tile(TILES - 1, 1)
            hT_copy(TILES - 1, 1)

        @block.gpsimd
        def _(pool):
            pool.wait_ge(const_in, 80)

            def rstd_of(n, s, mv, at, done, count):
                pool.wait_ge(mv, n + 1)
                pool.tensor_tensor(st[s][:, at:at + 1], st[s][:, at - 1:at], cst[0:N, C_POW + 2:C_POW + 3],
                                   ALU.add).then_inc(veps, 1)
                pool.wait_ge(veps, count)
                pool.tensor_tensor(st[s][:, at + 1:at + 2], st[s][:, at:at + 1], cst[0:N, C_POW:C_POW + 1],
                                   ALU.pow).then_inc(done, 1)

            def scatter(g):
                pool.wait_ge(weights, g + 1)
                pool.wait_ge(slots, g + 1)
                pool.wait_ge(row_done, 2 * g + 2)
                for k in range(GB):
                    n = 2 * g + k
                    for c, (row, slot, done) in enumerate(((row1, slot1, scat1), (row2, slot2, scat2))):
                        if k == 0 and not (isinstance(g, int) and g == 0):
                            pool.wait_ge(done, 32 * g)
                        pool.nop(nofuse=True)
                        pool.tensor_copy(row[k][:, 0:WT], rows[:, bass.ds(n, 1), 0:WT].rearrange("p a c -> p (a c)"))\
                            .then_inc(copied, 1)
                        pool.tensor_copy(row[k][:, WT:WT + 1], rs[:, 2 + c, k:k + 1]).then_inc(weighted, 1)
                        pool.wait_ge(copied, 4 * g + 2 * k + c + 1)
                        pool.wait_ge(weighted, 4 * g + 2 * k + c + 1)
                        pool.wait_ge(const_in, 80)
                        pool.nop(nofuse=True)
                        pool.indirect_dma_start(xs[:, :], bass.IndirectOffsetOnAxis(slot[:, k:k + 1], 0),
                                                row[k][:, :], None).then_inc(done, 16)

            def square_root(g):
                pool.wait_ge(softp, g + 1)
                pool.tensor_tensor(rt[:, SC, :], rt[:, SP, :], cst[0:N, C_POW + 1:C_POW + 2].broadcast_to([N, GE]),
                                   ALU.pow).then_inc(root, 1)

            def step(n, s, after, out, group):
                if after:
                    rstd_of(n + 1, 1 - s, mv1, 8, rstd1, 2 * n + 2)
                if out is not None:
                    scatter(out)
                if group is not None:
                    square_root(group)
                rstd_of(n, s, mv2, 12, rstd2, 2 * n + 3 if after else 2 * n + 2)
                pool.wait_ge(x2_done, n + 1)
                pool.nop(nofuse=True)
                pool.tensor_copy(rows[:, bass.ds(n, 1), 0:D], x2[s][:, :].unsqueeze(1)).then_inc(row_done, 1)

            rstd_of(0, 0, mv1, 8, rstd1, 1)
            step(0, 0, True, None, None)
            step(1, 1, True, None, None)
            step(2, 0, True, None, 0)
            step(3, 1, True, None, None)
            step(4, 0, True, 0, 1)
            step(5, 1, True, None, None)
            with pool.Fori(3, B // 2 - 1) as i:
                step(2 * i, 0, True, i - 2, i - 1)
                step(2 * i + 1, 1, True, None, None)
            step(B - 2, 0, True, B // 2 - 3, B // 2 - 2)
            step(B - 1, 1, False, None, None)
            scatter(B // 2 - 2)
            square_root(B // 2 - 1)
            scatter(B // 2 - 1)

            def add_rows(t, s):
                pool.wait_ge(meta_done, t + 1)
                pool.nop(nofuse=True)
                pool.tensor_copy(idx[s][:, :], meta[:, bass.ds(t, 1), 0]).then_inc(idx_done, 1)
                pool.wait_ge(idx_done, t + 1)
                pool.wait_ge(y_done, t + 1)
                if not (isinstance(t, int) and t == 0):
                    pool.wait_ge(y_out, 16 * t)
                pool.nop(nofuse=True)
                pool.indirect_dma_start(acc[:, :], bass.IndirectOffsetOnAxis(idx[s][:, 0:1], 0),
                                        yout[s][:, :], None, compute_op=ALU.add).then_inc(y_out, 16)

            pool.wait_ge(spare_out, 32)
            pool.wait_ge(acc_out[0], 8 * B)
            pool.wait_ge(acc_out[1], 8 * B)
            add_rows(0, 0)
            with pool.Fori(0, (TILES - 1) // 2) as i:
                add_rows(2 * i + 1, 1)
                add_rows(2 * i + 2, 0)
            add_rows(TILES - 1, 1)

        @block.vector
        def _(dve):
            V = nc.vector
            V.memset(filler[:, 0:D], 0.0).then_inc(fill_done, 1)
            V.memset(filler[:, WT:WT + 1], 0.0).then_inc(fill_done, 1)
            for s in range(2):
                V.memset(oT[s][DC:DC + 1, 1, :], 1.0).then_inc(ones_done, 1)
                V.memset(va[s][:, :, HD:VW], 1.0).then_inc(ones_done, 1)
            dve.wait_ge(const_in, 80)
            V.tensor_copy(filler[:, ID:ID + 1], cst[:, C_FILL:C_FILL + 1]).then_inc(fill_done, 1)
            V.tensor_copy(rows[:, :, ID], cst[0:N, C_TOK:C_TOK + B]).then_inc(ones_done, 1)
            V.tensor_copy(run[:, :], cst[0:N, C_REG:C_REG + E]).then_inc(ones_done, 1)
            V.tensor_tensor(clsrow, clsrow, small_sb[:, 2 * D:3 * D], ALU.add).then_inc(cls_done, 1)
            for t in range(ET):
                w = min(P, B * NPATCH - t * P)
                dve.wait_ge(emb_ps, t + 1)
                V.tensor_tensor(emb_sb[0:w, t, :], bank(t)[0:w, 0:D], pr_sb[0:w, t, :], ALU.add).then_inc(emb_done, 1)

            def norm1(n, s, times):
                dve.wait_ge(h_in[s], times)
                V.bn_stats(st[s][:, 0:6], h[s][:, :]).then_inc(bn1, 1)
                dve.wait_ge(bn1, n + 1)
                dve.nop(nofuse=True)
                V.bn_aggr(st[s][:, 6:8], st[s][:, 0:6]).then_inc(mv1, 1)

            def norm1_end(n, s):
                dve.wait_ge(rstd1, n + 1)
                V.tensor_scalar(xh[s][:, 0:D], h[s][:, :], st[s][:, 6:7], st[s][:, 9:10], ALU.subtract, ALU.mult)\
                    .then_inc(xn_done, 1)

            def gate_max(n, s):
                dve.wait_ge(lora_ps, n + 1)
                V.tensor_reduce(st[s][:, 16:17], bank(0)[0:N, E * R:NLG], AX.X, ALU.max, negate=True)\
                    .then_inc(gmax, 1)

            def gated(n, s):
                dve.wait_ge(gexp, n + 1)
                V.reciprocal(st[s][:, 18:19], st[s][:, 17:18]).then_inc(grcp, 1)
                dve.wait_ge(grcp, n + 1)
                V.scalar_tensor_tensor(xh[s][:, D:2 * P].rearrange("p (e r) -> p e r", r=R),
                                       bank(0)[0:N, 0:E * R].rearrange("p (e r) -> p e r", r=R), st[s][:, 18:19],
                                       st[s][:, 20:20 + E].unsqueeze(2).broadcast_to([N, E, R]),
                                       ALU.mult, ALU.mult).then_inc(hg_done, 1)

            def qkv_bias(n, s):
                for b, dst, done_ps, done in ((1, qT, q_ps, q_done), (2, kT, k_ps, k_done)):
                    dve.wait_ge(done_ps, n + 1)
                    V.tensor_tensor(dst[s].rearrange("p (g m) -> p g m", g=NG),
                                    bank(b)[:, 0:NG * N].rearrange("p (g m) -> p g m", g=NG),
                                    bqk_sb[:, (b - 1) * NG:b * NG].unsqueeze(2).broadcast_to([P, NG, N]),
                                    ALU.add).then_inc(done, 1)
                dve.wait_ge(v_ps, n + 1)
                V.tensor_tensor(va[s][:, :, 0:HD], bank(3)[0:N, 0:D].rearrange("p (h d) -> p h d", d=HD),
                                bv_sb[:, :].rearrange("p (h d) -> p h d", d=HD), ALU.add).then_inc(v_done, 1)

            def softmax(n, s, half):
                dve.wait_ge(s_ps, 2 * n + half + 1)
                sv = ps[0:N, 2 * half:2 * half + 2, 0:NG * N].rearrange("p j (g k) -> p j g k", g=NG)
                mx = smx[s][:, 6 * half:6 * half + 6].rearrange("p (j g) -> p j g", j=2)
                V.tensor_reduce(mx, sv, AX.X, ALU.max).then_inc(smax, 1)
                dve.wait_ge(smax, 2 * n + half + 1)
                V.tensor_tensor(prob[s][:, half * 6 * N:(half + 1) * 6 * N].rearrange("p (j g k) -> p j g k", j=2, g=NG),
                                sv, mx.unsqueeze(3).broadcast_to([N, 2, NG, N]), ALU.subtract).then_inc(ssub, 1)

            def attend_end(n, s):
                dve.wait_ge(pv_ps, n + 1)
                ov = bank(0)[0:N, 0:H * VW].rearrange("p (h d) -> p h d", d=VW)
                V.reciprocal(smx[s][:, H:2 * H], ov[:, :, HD]).then_inc(ssum, 1)
                dve.wait_ge(ssum, n + 1)
                V.tensor_tensor(o[s][:, :].rearrange("p (h d) -> p h d", d=HD), ov[:, :, 0:HD],
                                smx[s][:, H:2 * H].unsqueeze(2).broadcast_to([N, H, HD]), ALU.mult).then_inc(o_done, 1)

            def residual(n, s, times):
                if times is not None:
                    dve.wait_ge(acc_out[s], times)
                dve.wait_ge(proj_ps, n + 1)
                V.tensor_tensor(h2[s][:, :], bank(3)[0:N, 0:D], h[s][:, :], ALU.add).then_inc(h2_done, 1)
                dve.wait_ge(h2_done, n + 1)
                V.bn_stats(st[s][:, 0:6], h2[s][:, :]).then_inc(bn2, 1)
                dve.wait_ge(bn2, n + 1)
                dve.nop(nofuse=True)
                V.bn_aggr(st[s][:, 10:12], st[s][:, 0:6]).then_inc(mv2, 1)

            def norm2(n, s):
                dve.wait_ge(rstd2, n + 1)
                V.tensor_scalar(x2[s][:, :], h2[s][:, :], st[s][:, 10:11], st[s][:, 13:14], ALU.subtract, ALU.mult)\
                    .then_inc(x2_done, 1)

            def logit_copy(n, s):
                dve.wait_ge(logit_ps, n + 1)
                V.tensor_copy(rt[:, LG, s * E:(s + 1) * E], bank(6)[0:N, 2 * N:2 * N + E]).then_inc(logit_done, 1)

            def shared_hidden(n, half):
                dve.wait_ge(act_done, 2 * n + half + 1)
                V.scalar_tensor_tensor(gbuf[half][0:N, :], gbuf[half][0:N, :], 1.0, bank(4)[0:N, 0:HALF],
                                       ALU.add, ALU.mult).then_inc(gs_done, 1)
                dve.wait_ge(u_ps, 2 * n + half + 1)
                V.tensor_scalar(ubuf[half][0:N, :], bank(5)[0:N, 0:HALF], -LIMIT, LIMIT, ALU.max, ALU.min)\
                    .then_inc(clip_done, 1)
                dve.wait_ge(gs_done, 2 * n + half + 1)
                dve.wait_ge(clip_done, 2 * n + half + 1)
                V.scalar_tensor_tensor(hbuf[half][0:N, :], gbuf[half][0:N, :], 2 * SILU_LIMIT, ubuf[half][0:N, :],
                                       ALU.min, ALU.mult).then_inc(hh_done, 1)

            def shared_sum(n, s):
                dve.wait_ge(y_ps, n + 1)
                dve.wait_ge(x2_done, n + 1)
                V.tensor_tensor(h2[s][:, :], bank(7)[0:N, 0:D], h2[s][:, :], ALU.add).then_inc(sum_done, 1)

            steps = [0]

            def link(g, ins):
                steps[0] += 1
                ins.then_inc(rstep, 1)
                dve.wait_ge(rstep, RSTEPS * g + steps[0])

            def rv(k):
                return rt[:, k, :].rearrange("p (n e) -> p n e", e=E)

            def over_e(a):
                return a.unsqueeze(2).broadcast_to([N, GB, E])

            iota = cst[0:N, C_IOTA:C_IOTA + GE]

            def absolute(g):
                V.scalar_tensor_tensor(rt[:, TMP, :], rt[:, LG, :], -1.0, rt[:, LG, :], ALU.mult, ALU.max).then_inc(absl, 1)

            def softplus_a(g):
                steps[0] = 0
                dve.wait_ge(uexp, g + 1)
                link(g, V.tensor_scalar(rt[:, Z, :], rt[:, U, :], 2.0, None, ALU.add))
                link(g, V.reciprocal(rt[:, Z, :], rt[:, Z, :]))
                link(g, V.tensor_tensor(rt[:, Z, :], rt[:, Z, :], rt[:, U, :], ALU.mult))
                link(g, V.tensor_tensor(rt[:, Z2, :], rt[:, Z, :], rt[:, Z, :], ALU.mult))
                link(g, V.tensor_scalar(rt[:, Q, :], rt[:, Z2, :], 1.0 / 17, 1.0 / 15, ALU.mult, ALU.add))
                link(g, V.tensor_tensor(rt[:, Q, :], rt[:, Q, :], rt[:, Z2, :], ALU.mult))
                for c in (13, 11, 9):
                    link(g, V.scalar_tensor_tensor(rt[:, Q, :], rt[:, Q, :], 1.0 / c, rt[:, Z2, :], ALU.add, ALU.mult))

            def softplus_b(g):
                for c in (7, 5, 3):
                    link(g, V.scalar_tensor_tensor(rt[:, Q, :], rt[:, Q, :], 1.0 / c, rt[:, Z2, :], ALU.add, ALU.mult))
                link(g, V.scalar_tensor_tensor(rt[:, Q, :], rt[:, Q, :], 1.0, rt[:, Z, :], ALU.add, ALU.mult))
                link(g, V.tensor_scalar(rt[:, Z, :], rt[:, LG, :], 0.0, None, ALU.max))
                V.scalar_tensor_tensor(rt[:, SP, :], rt[:, Q, :], 2.0, rt[:, Z, :], ALU.mult, ALU.add).then_inc(softp, 1)

            def choose(g, mask, col):
                link(g, V.tensor_reduce(rs[:, col, :], rv(A), AX.X, ALU.max))
                link(g, V.tensor_tensor(rv(mask), rv(A), over_e(rs[:, col, :]), ALU.is_ge))
                link(g, V.tensor_tensor(rt[:, mask, :], rt[:, mask, :], iota, ALU.mult))
                link(g, V.tensor_reduce(rs[:, col, :], rv(mask), AX.X, ALU.min))
                link(g, V.tensor_tensor(rv(mask), iota.rearrange("p (n e) -> p n e", e=E), over_e(rs[:, col, :]), ALU.is_equal))

            def first_choice(g):
                dve.wait_ge(root, g + 1)
                link(g, V.tensor_tensor(rt[:, A, :], rt[:, SC, :], cst[0:N, C_BIAS:C_BIAS + GE], ALU.add))
                choose(g, M1, 0)
                link(g, V.scalar_tensor_tensor(rt[:, A, :], rt[:, M1, :], -3.0e38, rt[:, A, :], ALU.mult, ALU.add))

            def second_choice(g):
                choose(g, M2, 1)
                V.tensor_tensor(rt[:, PICK, :], rt[:, M1, :], rt[:, M2, :], ALU.add).then_inc(picks, 1)

            def shares(g):
                if not (isinstance(g, int) and g == 0):
                    dve.wait_ge(weighted, 4 * g)
                link(g, V.tensor_tensor(rt[:, W0, :], rt[:, M1, :], rt[:, SC, :], ALU.mult))
                link(g, V.tensor_tensor(rt[:, W1, :], rt[:, M2, :], rt[:, SC, :], ALU.mult))
                link(g, V.tensor_reduce(rs[:, 2:4, :], rt[:, W0:W0 + 2, :].rearrange("p a (n e) -> p a n e", e=E), AX.X, ALU.add))
                link(g, V.tensor_tensor(rs[:, 4, :], rs[:, 2, :], rs[:, 3, :], ALU.add))
                link(g, V.tensor_scalar(rs[:, 4, :], rs[:, 4, :], 1e-6, None, ALU.max))
                link(g, V.reciprocal(rs[:, 4, :], rs[:, 4, :]))
                V.tensor_tensor(rs[:, 2:4, :], rs[:, 2:4, :], rs[:, 4, :].unsqueeze(1).broadcast_to([N, 2, GB]), ALU.mult)\
                    .then_inc(weights, 1)

            def place_rows(g):
                dve.wait_ge(rank_ps, g + 1)
                V.tensor_copy(rt[:, W2:W2 + 2, :].rearrange("p a b -> p (a b)"), bank(5)[0:N, 0:2 * GE]).then_inc(rank_copied, 1)
                dve.wait_ge(rank_copied, g + 1)
                if not (isinstance(g, int) and g == 0):
                    dve.wait_ge(scat2, 32 * g)
                    dve.wait_ge(scat1, 32 * g)
                for k in range(GB):
                    part = slice(k * E, (k + 1) * E)
                    link(g, V.tensor_tensor(rt[:, RANK, part], rt[:, W2, part], run[:, :], ALU.add))
                    link(g, V.tensor_tensor(run[:, :], run[:, :], rt[:, W3, part], ALU.add))
                link(g, V.tensor_tensor(rt[:, W0, :], rt[:, M1, :], rt[:, RANK, :], ALU.mult))
                link(g, V.tensor_tensor(rt[:, W1, :], rt[:, M2, :], rt[:, RANK, :], ALU.mult))
                link(g, V.tensor_reduce(rs[:, 6:8, :], rt[:, W0:W0 + 2, :].rearrange("p a (n e) -> p a n e", e=E), AX.X, ALU.add))
                V.tensor_copy(slot1[:, :], rs[:, 6, :])
                V.tensor_copy(slot2[:, :], rs[:, 7, :]).then_inc(slots, 1)
                assert steps[0] == RSTEPS

            def step(n, s, before, after, times, stored, place, soft, pick):
                z = 1 - s
                if after:
                    norm1(n + 1, z, times)
                if place is not None:
                    steps[0] = PLACED
                    shares(place)
                    place_rows(place)
                if after:
                    norm1_end(n + 1, z)
                softmax(n, s, 0)
                softmax(n, s, 1)
                if before:
                    logit_copy(n - 1, z)
                    if soft is not None:
                        dve.wait_ge(logit_done, n)
                        absolute(soft)
                    shared_hidden(n - 1, 0)
                if soft is not None:
                    softplus_a(soft)
                if pick is not None:
                    steps[0] = SOFT
                    first_choice(pick)
                attend_end(n, s)
                if soft is not None:
                    softplus_b(soft)
                if before:
                    shared_hidden(n - 1, 1)
                if pick is not None:
                    second_choice(pick)
                if after:
                    gate_max(n + 1, z)
                residual(n, s, stored)
                if after:
                    gated(n + 1, z)
                norm2(n, s)
                if before:
                    shared_sum(n - 1, z)
                if after:
                    qkv_bias(n + 1, z)

            norm1(0, 0, 48)
            norm1_end(0, 0)
            gate_max(0, 0)
            gated(0, 0)
            qkv_bias(0, 0)
            step(0, 0, False, True, 48, None, None, None, None)
            step(1, 1, True, True, 96, None, None, None, None)
            step(2, 0, True, True, 96, 16, None, 0, None)
            step(3, 1, True, True, 144, 16, None, None, 0)
            step(4, 0, True, True, 144, 32, 0, 1, None)
            step(5, 1, True, True, 192, 32, None, None, 1)
            with dve.Fori(3, B // 2 - 1) as i:
                step(2 * i, 0, True, True, 48 * i + 48, 16 * i, i - 2, i - 1, None)
                step(2 * i + 1, 1, True, True, 48 * i + 96, 16 * i, None, None, i - 1)
            last = B // 2 - 1
            step(B - 2, 0, True, True, 48 * last + 48, 16 * last, last - 2, last - 1, None)
            step(B - 1, 1, True, False, None, 16 * last, None, None, last - 1)

            steps[0] = PLACED
            shares(last - 1)
            place_rows(last - 1)
            logit_copy(B - 1, 1)
            dve.wait_ge(logit_done, B)
            absolute(last)
            shared_hidden(B - 1, 0)
            softplus_a(last)
            softplus_b(last)
            shared_hidden(B - 1, 1)
            first_choice(last)
            second_choice(last)
            shares(last)
            shared_sum(B - 1, 1)
            place_rows(last)

            ends = [0]

            def then(ins):
                ends[0] += 1
                ins.then_inc(rstep, 1)
                dve.wait_ge(rstep, RSTEPS * (B // 2) + ends[0])

            then(V.tensor_tensor(off[:, 5, :], run[:, :], cst[0:N, C_REG:C_REG + E], ALU.subtract))
            jc = jcmp[:, 0:E * MOST].rearrange("p (e j) -> p e j", e=E)
            then(V.tensor_tensor(jc, off[:, 5, :].unsqueeze(2).broadcast_to([N, E, MOST]),
                                 cst[0:N, C_J:C_J + E * MOST].rearrange("p (e j) -> p e j", e=E), ALU.is_gt))
            then(V.tensor_reduce(off[:, 0, :], jc, AX.X, ALU.add))
            for k, sh in enumerate((1, 2, 4)):
                then(V.tensor_copy(off[:, k + 1, 0:sh], off[:, k, 0:sh]))
                then(V.tensor_tensor(off[:, k + 1, sh:], off[:, k, sh:], off[:, k, 0:E - sh], ALU.add))
            te = jcmp[:, 0:LOADS * E].rearrange("p (t e) -> p t e", e=E)
            then(V.tensor_tensor(te, cst[0:N, C_T:C_T + LOADS * E].rearrange("p (t e) -> p t e", e=E),
                                 off[:, 3, :].unsqueeze(1).broadcast_to([N, LOADS, E]), ALU.is_ge))
            then(V.tensor_reduce(tv[:, 0, :], te, AX.X, ALU.add))
            then(V.tensor_tensor(te, te, off[:, 0, :].unsqueeze(1).broadcast_to([N, LOADS, E]), ALU.mult))
            then(V.tensor_reduce(tv[:, 1, :], te, AX.X, ALU.add))
            then(V.tensor_tensor(tv[:, 1, :], cst[0:N, C_TT:C_TT + LOADS], tv[:, 1, :], ALU.subtract))
            then(V.tensor_scalar(tv[:, 1, :], tv[:, 1, :], float(P), None, ALU.mult))
            then(V.scalar_tensor_tensor(tv[:, 1, :], tv[:, 0, :], float(REGION), tv[:, 1, :], ALU.mult, ALU.add))
            then(V.tensor_copy(rtab[:, :], tv[0:1, 1, :]))
            then(V.tensor_scalar(tv[:, 1, :], tv[:, 0, :], float(E - 1), 1.0, ALU.min, ALU.add))
            then(V.tensor_copy(etab[:, 0:LOADS], tv[0:1, 1, :]))
            then(V.tensor_scalar(tv[:, 2, :], tv[:, 0, :], float(E - LATE), None, ALU.is_ge))
            then(V.tensor_scalar(tv[:, 2, :], tv[:, 2, :], 48.0 * LATE, 48.0 * (E - LATE), ALU.mult, ALU.add))
            then(V.tensor_copy(wtab[:, :], tv[0:1, 2, :]))
            V.tensor_copy(ftab[:, :], run[0:1, :]).then_inc(tables, 1)

            def hidden(t, half):
                dve.wait_ge(ru_ps, 2 * t + half + 1)
                V.tensor_scalar(ubuf[half][:, :], ps[:, 2 + half, 0:HALF], -LIMIT, LIMIT, ALU.max, ALU.min)\
                    .then_inc(rclip_done, 1)
                dve.wait_ge(rclip_done, 2 * t + half + 1)
                dve.wait_ge(silu_done, 2 * t + half + 1)
                V.scalar_tensor_tensor(hbuf[half][:, :], gbuf[half][:, :], SILU_LIMIT, ubuf[half][:, :],
                                       ALU.min, ALU.mult).then_inc(rhh_done, 1)

            def meta_copy(t, s, times):
                dve.wait_ge(x_in[s], times)
                V.tensor_copy(meta[:, bass.ds(t, 1), :], xin[s][:, ID:ROW].unsqueeze(1)).then_inc(meta_done, 1)

            def result(t, s):
                dve.wait_ge(ry_ps, t + 1)
                if not (isinstance(t, int) and t < 2):
                    dve.wait_ge(y_out, 16 * t - 16)
                V.tensor_scalar(yout[s][:, :], ps[:, 6, 0:D], meta[:, bass.ds(t, 1), 1], None, ALU.mult)\
                    .then_inc(y_done, 1)

            meta_copy(0, 0, 16)
            hidden(0, 0)
            meta_copy(1, 1, 16)
            hidden(0, 1)

            def tile(t, s, times):
                hidden(t, 0)
                meta_copy(t + 1, 1 - s, times)
                result(t - 1, 1 - s)
                hidden(t, 1)

            tile(1, 1, 32)
            tile(2, 0, 32)
            with dve.Fori(1, (TILES - 1) // 2) as i:
                tile(2 * i + 1, 1, 16 * i + 32)
                tile(2 * i + 2, 0, 16 * i + 32)
            tile(TILES - 1, 1, 8 * (LOADS + 1))
            result(TILES - 1, 1)


SOFT = 14
PLACED = SOFT + 7 + 5
RSTEPS = PLACED + 6 + 7


def kernel(**inputs):
    import numpy as np
    import concourse.bacc as bacc
    from concourse import mybir as _mybir
    from concourse.bass_utils import run_bass_kernel_spmd as run

    a = {k: np.asarray(v) for k, v in inputs.items()}
    f32 = np.float32

    x = a["x"].reshape(B, 3, 6, 16, 6, 16).transpose(1, 3, 5, 0, 2, 4).reshape(6, P, B * NPATCH)
    patches = x.transpose(1, 0, 2)
    proj_w = a["L0_tok_proj_w"].T.reshape(6, P, D).transpose(1, 0, 2)
    pos = a["L0_tok_pos_embedding"].reshape(NEMB, D)
    pos_rows = pos[1 + np.arange(ET * P) % NPATCH].reshape(ET, P, D).transpose(1, 0, 2)
    small = np.concatenate([a["L0_tok_proj_b"], a["L0_tok_cls_token"].reshape(D), pos[0]])[None]

    def heads_apart(m):
        out = np.zeros((m.shape[0], LOFF), f32)
        for part in range(2):
            to = out[:, part * QG:(part + 1) * QG].reshape(-1, NG, NJ, 32)
            to[:, :, :, 0:HD] = m[:, part * D:(part + 1) * D].reshape(-1, NG, NJ, HD)
        out[:, VOFF:] = m[:, 2 * D:]
        return out

    wa = np.zeros((2 * P, NWA), f32)
    wa[0:D, 0:LOFF] = heads_apart(a["L0_attn_qkv_w"].T)
    wa[D:, 0:LOFF] = heads_apart(a["L0_attn_lora_b"].reshape(E * R, 3 * D))
    wa[0:D, LOFF:LOFF + E * R] = a["L0_attn_lora_a"].transpose(1, 0, 2).reshape(D, E * R)
    wa[0:D, LOFF + E * R:] = a["L0_attn_gate_w"].T
    wa = wa.reshape(2, P, NWA).transpose(1, 0, 2)
    bias = heads_apart(a["L0_attn_qkv_b"][None])[0]
    bqk = bias[0:VOFF].reshape(2 * NG, P).T
    bv = np.broadcast_to(bias[VOFF:], (N, D))
    out_w = np.zeros((DC + 1, 2, D), f32)
    for c in range(2):
        out_w[0:DC, c] = a["L0_attn_proj_w"].T[c * DC:(c + 1) * DC]
    out_w[DC, 1] = a["L0_attn_proj_b"]
    gate_w = a["L0_ffn_gate_w"].reshape(2, DC, E).transpose(1, 0, 2)

    p = np.arange(P)
    consts = np.zeros((P, C_ALL), f32)
    consts[:, C_ID:C_ID + P] = np.eye(P)
    consts[:, C_TRI:C_TRI + N] = p[:, None] < np.arange(N)[None, :]
    consts[:, C_ONE:C_ONE + P] = 1
    consts[:, C_IOTA:C_IOTA + GE] = np.tile(np.arange(E) - E, GB)
    consts[:, C_J:C_J + E * MOST] = np.tile(P * np.arange(MOST), E)
    consts[:, C_T:C_T + LOADS * E] = np.repeat(np.arange(LOADS), E)
    consts[:, C_TT:C_TT + LOADS] = np.arange(LOADS)
    consts[:, C_POW:C_POW + 3] = (-0.5, 0.5, EPS)
    consts[:, C_TOK:C_TOK + B] = N * np.arange(B)[None, :] + p[:, None]
    consts[:, C_FILL] = T + p
    consts[:, C_REG:C_REG + E] = REGION * np.arange(E)
    consts[:, C_BIAS:C_BIAS + GE] = np.tile(a["L0_ffn_gate_bias"], GB)

    nc = bacc.Bacc("TRN2", target_bir_lowering=False, num_devices=1)
    arrays = {
        "patches": patches, "txt": a["txt"], "proj_w": proj_w, "pos_rows": pos_rows, "small": small, "wa": wa,
        "bqk": bqk, "bv": bv, "out_w": out_w, "gate_w": gate_w, "consts": consts, "w1": a["L0_ffn_w1"],
        "w2": a["L0_ffn_w2"], "w3": a["L0_ffn_w3"], "w1s": a["L0_ffn_w1s"], "w2s": a["L0_ffn_w2s"], "w3s": a["L0_ffn_w3s"],
    }
    arrays = {f"in_{k}": np.ascontiguousarray(v) for k, v in arrays.items()}
    args = [nc.dram_tensor(k, v.shape, _mybir.dt.from_np(v.dtype), kind="ExternalInput").ap() for k, v in arrays.items()]
    args.append(nc.dram_tensor("acc", (T + P, D), F32, kind="ExternalOutput").ap())
    args.append(nc.dram_tensor("xs", (E * REGION + SPARE * P, ROW), F32, kind="Internal").ap())
    args.append(nc.dram_tensor("emb", (B * NPATCH, D), F32, kind="Internal").ap())
    program(nc, *args)
    r = run(nc, [arrays], core_ids=[0])
    return r.results[0]["acc"][0:T].reshape(B, N, D)
```

```python
from contextlib import ExitStack

import concourse.bass as bass
from concourse import mybir

F32 = mybir.dt.float32
U32 = mybir.dt.uint32
I32 = mybir.dt.int32
ALU = mybir.AluOpType
ACT = mybir.ActivationFunctionType
AX = mybir.AxisListType

B, NPATCH, NTXT, D = 16, 36, 77, 192
NEMB = NPATCH + 1
N = NEMB + NTXT
T = B * N
KP = 768
H, HD, NG, NJ = 12, 16, 3, 4
E, R, I = 8, 8, 768
DC = D // 2
LIMIT = 10.0
SILU_LIMIT = 9.999546021312976
EPS = 1e-5
SCALE = HD ** -0.5
QG = NG * 128
QOFF, KOFF, VOFF, LOFF = 0, QG, 2 * QG, 2 * QG + D
NLG = E * R + E
NWA = LOFF + NLG
VW = HD + 1

P = 128
PP = D - P
MOST = -(-T // P)
TILES = (2 * T + E * (P - 1)) // P
SPARE = TILES + 1 - -(-2 * T // P)
LOADS = TILES + 1
ROW = D + 2
ID, WT = D, D + 1
HALF = I // 2
KH = HALF // P
LATE = 4
ET = -(-B * NPATCH // P)
GB = 2
GE = GB * E
FILL = -(-(2 * GB * N + P) // P)
REGION = -(-(T - 2 * GB * N + FILL * P) // P) * P

C_ID, C_TRI, C_ONE, C_IOTA = 0, P, P + N, 2 * P + N
C_J = C_IOTA + GE
C_T = C_J + E * MOST
C_TT = C_T + LOADS * E
C_POW = C_TT + LOADS
C_TOK = C_POW + 3
C_FILL = C_TOK + B
C_REG = C_FILL + 1
C_BIAS = C_REG + E
C_ALL = C_BIAS + GE


def load_expert(queue, w1, w2, w3, w13, wdn, done, e):
    for src, at in ((w1, 0), (w3, I)):
        queue.dma_start(w13[0:DC, bass.ds(e, 1), :].rearrange("p a (c m) -> p (a c) m", c=2)[:, :, at:at + I],
                        src[bass.ds(e, 1)].rearrange("a (c p) i -> p (a c) i", c=2)).then_inc(done, 16)
    queue.dma_start(wdn[:, bass.ds(e, 1), :].rearrange("p a (k d) -> p (a k) d", d=D),
                    w2[bass.ds(e, 1)].rearrange("a (k p) d -> p (a k) d", p=P)).then_inc(done, 16)


def program(nc, patches, txt, proj_w, pos_rows, small, wa, bqk, bv, out_w, gate_w, consts, w1, w2, w3, w1s, w2s, w3s,
            acc, xs, emb):
    with ExitStack() as ctx:
        def sb(name, shape, dt=F32):
            return ctx.enter_context(nc.sbuf_tensor(name, shape, dt))

        def sem(name):
            return ctx.enter_context(nc.semaphore(name))

        w13 = sb("w13", [P, E, 2 * 2 * I])
        wdn = sb("wdn", [P, E, (I // P) * D])
        w13s = sb("w13s", [DC, 2, 2 * I + E])
        wdns = sb("wdns", [P, (I // P) * D])
        late13 = w13[:, E - LATE:, :].rearrange("p a b -> p (a b)")
        late2 = wdn[:, E - LATE:, :].rearrange("p a b -> p (a b)")
        used = [0, 0]

        def lend(k, rows_, size):
            part = (late13, late2)[k][0:rows_, used[k]:used[k] + size]
            used[k] += size
            assert used[k] <= LATE * (4 * I, (I // P) * D)[k]
            return part

        prob = [lend(0, N, H * N) for _ in range(2)]
        probT = [lend(0, N, H * N) for _ in range(2)]
        qT = [lend(0, P, NG * N) for _ in range(2)]
        kT = [lend(0, P, NG * N) for _ in range(2)]
        patch_sb = lend(0, P, 6 * B * NPATCH).rearrange("p (k m) -> p k m", k=6)
        wa_sb = lend(1, P, 2 * NWA).rearrange("p (c n) -> p c n", c=2)
        pw_sb = lend(1, P, 6 * D).rearrange("p (k d) -> p k d", k=6)
        pr_sb = lend(1, P, ET * D).rearrange("p (k d) -> p k d", k=ET)

        cst = sb("cst", [P, C_ALL])
        small_sb = sb("small_sb", [1, 3 * D])
        ow_sb = sb("ow_sb", [DC + 1, 2, D])
        bqk_sb = sb("bqk_sb", [P, 2 * NG])
        bv_sb = sb("bv_sb", [N, D])
        rows = sb("rows", [N, B, ROW])
        row1 = [sb(f"row1_{s}", [N, ROW]) for s in range(2)]
        row2 = [sb(f"row2_{s}", [N, ROW]) for s in range(2)]
        filler = sb("filler", [P, ROW])
        x2 = [sb(f"x2{s}", [N, D]) for s in range(2)]
        h = [sb(f"h{s}", [N, D]) for s in range(2)]
        h2 = [sb(f"h2{s}", [N, D]) for s in range(2)]
        xh = [sb(f"xh{s}", [N, 2 * P]) for s in range(2)]
        xT1 = [lend(0, P, 2 * N).rearrange("p (c n) -> p c n", c=2) for _ in range(2)]
        st = [sb(f"st{s}", [N, 32]) for s in range(2)]
        va = [sb(f"va{s}", [N, H, VW]) for s in range(2)]
        smx = [sb(f"smx{s}", [N, 2 * H]) for s in range(2)]
        o = [sb(f"o{s}", [N, D]) for s in range(2)]
        oT = [lend(0, DC + 1, 2 * N).rearrange("p (c n) -> p c n", c=2) for _ in range(2)]
        x2T = [sb(f"x2T{s}", [DC, 2, N]) for s in range(2)]
        rt = sb("rt", [N, 18, GE])
        rs = sb("rs", [N, 8, GB])
        run = sb("run", [N, E])
        off = sb("off", [N, 6, E])
        jcmp = sb("jcmp", [N, LOADS * E])
        tv = sb("tv", [N, 3, LOADS])
        slots_of = [[sb(f"slots{k}_{c}", [N, GB], U32) for c in range(2)] for k in range(2)]
        etab = sb("etab", [1, LOADS + 1], I32)
        rtab = sb("rtab", [1, LOADS], I32)
        wtab = sb("wtab", [1, LOADS], I32)
        ftab = sb("ftab", [1, E], I32)

        xin = [sb(f"xin{s}", [P, ROW]) for s in range(2)]
        xT = [sb(f"xT{s}", [DC, 2, P]) for s in range(2)]
        meta = sb("meta", [P, LOADS, 2])
        gbuf = [sb(f"gbuf{i}", [P, HALF]) for i in range(2)]
        ubuf = [sb(f"ubuf{i}", [P, HALF]) for i in range(2)]
        hbuf = [sb(f"hbuf{i}", [P, HALF]) for i in range(2)]
        hT = [sb(f"hT{i}", [P, KH, P]) for i in range(2)]
        yout = [sb(f"yout{s}", [P, D]) for s in range(2)]
        idx = [sb(f"idx{s}", [P, 1], U32) for s in range(2)]
        emb_sb = lend(0, P, ET * D).rearrange("p (k d) -> p k d", k=ET)
        last_rows = [[[row1[k], row2[k]] for k in range(GB)], [[xh[0], xh[1]], [xin[0][0:N, :], xin[1][0:N, :]]]]
        clsrow = small_sb[:, D:2 * D]

        ps = ctx.enter_context(nc.psum_tensor("ps", [P, 8, 512], F32))
        ident = cst[:, C_ID:C_ID + P]
        LG, U, Z, Z2, Q, SP, SC, A, AM, M1, M2, PICK, RANK, TMP, W0, W1, W2, W3 = range(18)

        def bank(b):
            return ps[:, b, :]

        const_in, patch_in, wa_in, w_shared, w_in = (sem(x) for x in ("const_in", "patch_in", "wa_in", "w_shared", "w_in"))
        h_in = [sem(f"h_in{s}") for s in range(2)]
        emb_ps, emb_done, first_emb_out, emb_out = (sem(x) for x in ("emb_ps", "emb_done", "first_emb_out", "emb_out"))
        cls_done, ones_done = sem("cls_done"), sem("ones_done")
        xT_ps, lora_ps, hgT_ps, q_ps, k_ps, v_ps = (sem(x) for x in ("xT_ps", "lora_ps", "hgT_ps", "q_ps", "k_ps", "v_ps"))
        s_ps, pT_ps, pv_ps, oT_ps, proj_ps = (sem(x) for x in ("s_ps", "pT_ps", "pv_ps", "oT_ps", "proj_ps"))
        x2T_ps, logit_ps = sem("x2T_ps"), sem("logit_ps")
        bn1, mv1, veps, rstd1, xn_done, xT_done = (sem(x) for x in ("bn1", "mv1", "veps", "rstd1", "xn_done", "xT_done"))
        gmax, gexp, grcp, hg_done, hgT_done = (sem(x) for x in ("gmax", "gexp", "grcp", "hg_done", "hgT_done"))
        q_done, k_done, v_done = sem("q_done"), sem("k_done"), sem("v_done")
        smax, ssub, p_done, pT_done = (sem(x) for x in ("smax", "ssub", "p_done", "pT_done"))
        ssum, o_done, oT_done, h2_done = sem("ssum"), sem("o_done"), sem("oT_done"), sem("h2_done")
        bn2, mv2, rstd2, x2_done, x2T_done, row_done = (sem(x) for x in ("bn2", "mv2", "rstd2", "x2_done", "x2T_done", "row_done"))
        sum_done = sem("sum_done")
        acc_out = [sem(f"acc_out{s}") for s in range(2)]
        g_ps, u_ps, act_done, gs_done, clip_done, hh_done = (sem(x) for x in ("g_ps", "u_ps", "act_done", "gs_done", "clip_done", "hh_done"))
        hT_ps, hT_done, y_ps = sem("hT_ps"), sem("hT_done"), sem("y_ps")
        logit_done, absl, uexp, softp, root, picks = (sem(x) for x in ("logit_done", "absl", "uexp", "softp", "root", "picks"))
        rank_ps, rank_copied, slots, weights, rstep = (sem(x) for x in ("rank_ps", "rank_copied", "slots", "weights", "rstep"))
        copied, weighted, scat1, scat2 = sem("copied"), sem("weighted"), sem("scat1"), sem("scat2")
        tables, fill_done, fill_out, spare_out = sem("tables"), sem("fill_done"), sem("fill_out"), sem("spare_out")
        fill_from, staged = sem("fill_from"), sem("staged")
        x_in = [sem(f"x_in{s}") for s in range(2)]
        rxT_ps, rxT_done, meta_done = sem("rxT_ps"), sem("rxT_done"), sem("meta_done")
        rg_ps, ru_ps, silu_done, rclip_done, rhh_done = (sem(x) for x in ("rg_ps", "ru_ps", "silu_done", "rclip_done", "rhh_done"))
        rhT_ps, rhT_done, ry_ps, y_done, idx_done, y_out = (sem(x) for x in ("rhT_ps", "rhT_done", "ry_ps", "y_done", "idx_done", "y_out"))

        block = ctx.enter_context(nc.Block())

        @block.sync
        def _(sp):
            def load_h(n, s):
                sp.dma_start(h[s][0:1, :], clsrow).then_inc(h_in[s], 16)
                sp.dma_start(h[s][1:NEMB, :], emb[bass.ds(n * NPATCH, NPATCH), :]).then_inc(h_in[s], 16)
                sp.dma_start(h[s][NEMB:N, :], txt[bass.ds(n, 1)].rearrange("a t d -> (a t) d")).then_inc(h_in[s], 16)

            sp.dma_start(pw_sb, proj_w[:, :, :]).then_inc(const_in, 16)
            sp.dma_start(patch_sb[:, :, 0:P], patches[:, :, 0:P]).then_inc(const_in, 16)
            sp.dma_start(cst[:, :], consts[:, :]).then_inc(const_in, 16)
            sp.dma_start(small_sb[:, :], small[:, :]).then_inc(const_in, 16)
            sp.dma_start(pr_sb, pos_rows[:, :, :]).then_inc(const_in, 16)
            sp.dma_start(patch_sb[:, :, P:], patches[:, :, P:]).then_inc(patch_in, 16)
            for dst, src in ((wa_sb, wa), (w13s[:, :, HALF:HALF + E], gate_w), (ow_sb[:, :, :], out_w)):
                sp.dma_start(dst, src[:, :, :]).then_inc(wa_in, 16)
            sp.dma_start(bqk_sb[:, :], bqk[:, :]).then_inc(wa_in, 16)
            sp.dma_start(bv_sb[:, :], bv[:, :]).then_inc(wa_in, 16)
            sp.wait_ge(emb_done, 1)
            sp.dma_start(emb[0:P, :], emb_sb[:, 0, :]).then_inc(first_emb_out, 16)
            sp.wait_ge(cls_done, 1)
            sp.wait_ge(first_emb_out, 16)
            assert 2 * NPATCH <= P
            load_h(0, 0)
            load_h(1, 1)
            sp.wait_ge(emb_done, ET)
            full = B * NPATCH // P
            sp.dma_start(emb[P:full * P, :].rearrange("(k p) d -> p k d", p=P), emb_sb[:, 1:full, :]).then_inc(emb_out, 16)
            sp.dma_start(emb[full * P:, :], emb_sb[0:B * NPATCH - full * P, full, :]).then_inc(emb_out, 16)
            sp.wait_ge(fill_done, 3)
            sp.dma_start(xs[E * REGION:, :].rearrange("(t p) c -> p t c", p=P),
                         filler[:, :].unsqueeze(1).broadcast_to([P, SPARE, ROW])).then_inc(spare_out, 16)
            sp.dma_start(acc[T:T + P, :], filler[:, 0:D]).then_inc(spare_out, 16)
            sp.wait_ge(emb_out, 32)

            def store_sum(n, s):
                sp.wait_ge(sum_done, n + 1)
                sp.dma_start(acc[bass.ds(n * N, N), :], h2[s][:, :]).then_inc(acc_out[s], 16)

            def step(n, s, before, more):
                if before:
                    store_sum(n - 1, 1 - s)
                if more:
                    sp.wait_ge(h2_done, n + 1)
                    load_h(n + 2, s)

            step(0, 0, False, True)
            step(1, 1, True, True)
            with sp.Fori(1, B // 2 - 1) as i:
                step(2 * i, 0, True, True)
                step(2 * i + 1, 1, True, True)
            step(B - 2, 0, True, False)

            sp.wait_ge(fill_from, 1)
            for e in range(E):
                first = sp.value_load(ftab[0:1, e:e + 1], min_val=e * REGION, max_val=e * REGION + T - 2 * GB * N)
                sp.dma_start(xs[bass.ds(first, FILL * P), :].rearrange("(t p) c -> p t c", p=P),
                             filler[:, :].unsqueeze(1).broadcast_to([P, FILL, ROW])).then_inc(fill_out, 16)

            step(B - 1, 1, True, False)

            sp.wait_ge(proj_ps, B)
            sp.wait_ge(emb_out, 32)
            sp.wait_ge(w_in, 48 * (E - LATE))
            with sp.Fori(E - LATE, E) as e:
                load_expert(sp, w1, w2, w3, w13, wdn, w_in, e)

            def load_tile(t, s):
                row = sp.value_load(rtab[0:1, bass.ds(t, 1)], min_val=0, max_val=E * REGION + (SPARE - 1) * P)
                weights_in = sp.value_load(wtab[0:1, bass.ds(t, 1)], min_val=48 * (E - LATE), max_val=48 * E)
                if isinstance(t, int) and t == 0:
                    sp.wait_ge(spare_out, 32)
                    sp.wait_ge(fill_out, 16 * E)
                    sp.wait_ge(scat1, 16 * B)
                    sp.wait_ge(scat2, 16 * B)
                    sp.wait_ge(w_in, 48 * (E - LATE))
                sp.wait_ge(w_in, weights_in)
                sp.nop(nofuse=True)
                if not (isinstance(t, int) and t < 2):
                    sp.wait_ge(rxT_ps, t - 1)
                    sp.wait_ge(meta_done, t - 1)
                sp.nop(nofuse=True)
                sp.dma_start(xin[s][:, :], xs[bass.ds(row, P), :]).then_inc(x_in[s], 16)

            sp.wait_ge(tables, 1)
            load_tile(0, 0)
            load_tile(1, 1)
            with sp.Fori(1, LOADS // 2) as i:
                load_tile(2 * i, 0)
                load_tile(2 * i + 1, 1)
            load_tile(LOADS - 1, 0)
            sp.wait_ge(acc_out[0], 8 * B)
            sp.wait_ge(acc_out[1], 8 * B)
            sp.wait_ge(x_in[0], 8 * (LOADS + 1))
            sp.wait_ge(x_in[1], 8 * (LOADS - 1))
            sp.wait_ge(y_out, 16 * TILES)

        @block.tensor
        def _(pe):
            mm = nc.tensor.matmul

            pe.wait_ge(const_in, 80)
            for t in range(ET):
                w = min(P, B * NPATCH - t * P)
                if t == 1:
                    pe.wait_ge(patch_in, 16)
                for k in range(6):
                    mm(bank(t)[0:w, 0:D], patch_sb[:, k, t * P:t * P + w], pw_sb[:, k, :], start=(k == 0), stop=False)
                mm(bank(t)[0:w, 0:D], cst[0:1, C_ONE:C_ONE + w], small_sb[:, 0:D], start=False, stop=True)\
                    .then_inc(emb_ps, 1)

            def transpose_x(n, s):
                pe.wait_ge(xn_done, n + 1)
                nc.tensor.transpose(bank(2)[:, 0:N], xh[s][:, 0:P], ident[0:N, 0:N])
                nc.tensor.transpose(bank(2)[0:PP, N:2 * N], xh[s][:, P:D], ident[0:N, 0:N]).then_inc(xT_ps, 1)

            def lora_down(n, s):
                pe.wait_ge(xT_done, 2 * n + 2)
                out = bank(2)[0:N, 2 * N:2 * N + NLG]
                mm(out, xT1[s][:, 0, :], wa_sb[:, 0, LOFF:NWA], start=True, stop=False)
                mm(out, xT1[s][0:PP, 1, :], wa_sb[0:PP, 1, LOFF:NWA], start=False, stop=True).then_inc(lora_ps, 1)

            def transpose_hg(n, s):
                pe.wait_ge(hg_done, n + 1)
                nc.tensor.transpose(bank(2)[:, 0:N], xh[s][:, P:2 * P], ident[0:N, 0:N]).then_inc(hgT_ps, 1)

            def qk(n, s):
                pe.wait_ge(hgT_done, n + 1)
                for off0, b, done in ((QOFF, 1, q_ps), (KOFF, 2, k_ps)):
                    for g in range(NG):
                        cols = slice(off0 + g * P, off0 + (g + 1) * P)
                        for c in range(2):
                            last = mm(bank(b)[:, g * N:(g + 1) * N], wa_sb[:, c, cols], xT1[s][:, c, :],
                                      start=(c == 0), stop=(c == 1))
                    last.then_inc(done, 1)

            def values(n, s):
                for c in range(2):
                    last = mm(bank(5)[0:N, 2 * GE:2 * GE + D], xT1[s][:, c, :], wa_sb[:, c, VOFF:LOFF],
                              start=(c == 0), stop=(c == 1))
                last.then_inc(v_ps, 1)

            def scores(n, s, half):
                if half == 0:
                    pe.wait_ge(q_done, n + 1)
                    pe.wait_ge(k_done, n + 1)
                elif not (isinstance(n, int) and n == 0):
                    pe.wait_ge(h2_done, n)
                for g in range(NG):
                    for j in (2 * half, 2 * half + 1):
                        at = slice(32 * j, 32 * j + HD)
                        last = mm(bank(j)[0:N, g * N:(g + 1) * N], qT[s][at, g * N:(g + 1) * N],
                                  kT[s][at, g * N:(g + 1) * N], start=True, stop=True)
                last.then_inc(s_ps, 1)

            def transpose_p(n, s, half):
                pe.wait_ge(p_done, 2 * n + half + 1)
                for a in range(6 * half, 6 * half + 6):
                    last = nc.tensor.transpose(bank(a // 3)[0:N, (a % 3) * N:(a % 3 + 1) * N],
                                               prob[s][:, a * N:(a + 1) * N], ident[0:N, 0:N])
                last.then_inc(pT_ps, 1)

            def weigh_v(n, s, half, shared, after=False):
                at_head = ((0, 2, 3, 5), (0, 0, 2, 4))[half]
                for k in range(6):
                    a = 6 * half + k
                    for part, c in [divmod(m, 2) for m in range(4) if shared and at_head[m] == k]:
                        at = (HALF, I + HALF)[half] + E + part * D
                        large = mm(bank(4 + half)[0:N, part * D:(part + 1) * D], x2T[1 - s][:, c, :],
                                   w13s[:, c, at:at + D], start=(c == 0), stop=(c == 1))
                        if (part, c) == (1, 1):
                            large.then_inc((g_ps, u_ps)[half], 1)
                    if k == 0:
                        pe.wait_ge(pT_done, 2 * n + half + 1)
                        if half == 1 and after:
                            transpose_x(n + 1, 1 - s)
                    head = NJ * (a % NG) + a // NG
                    last = mm(bank(0)[0:N, head * VW:(head + 1) * VW], probT[s][:, a * N:(a + 1) * N],
                              va[s][:, head, :], start=True, stop=True)
                if half == 1:
                    last.then_inc(pv_ps, 1)

            def transpose_o(n, s):
                pe.wait_ge(o_done, n + 1)
                for c in range(2):
                    last = nc.tensor.transpose(bank(1)[0:DC, c * N:(c + 1) * N], o[s][:, c * DC:(c + 1) * DC],
                                               ident[0:N, 0:N])
                last.then_inc(oT_ps, 1)

            def project(n, s):
                pe.wait_ge(oT_done, n + 1)
                out = bank(3)[0:N, 0:D]
                mm(out, oT[s][0:DC, 0, :], ow_sb[0:DC, 0, :], start=True, stop=False)
                mm(out, oT[s][0:DC + 1, 1, :], ow_sb[0:DC + 1, 1, :], start=False, stop=True).then_inc(proj_ps, 1)

            def transpose_x2(n, s):
                pe.wait_ge(x2_done, n + 1)
                for c in range(2):
                    last = nc.tensor.transpose(bank(6)[0:DC, c * N:(c + 1) * N], x2[s][:, c * DC:(c + 1) * DC],
                                               ident[0:N, 0:N])
                last.then_inc(x2T_ps, 1)

            def route(n, s):
                pe.wait_ge(x2T_done, n + 1)
                for c in range(2):
                    last = mm(bank(6)[0:N, 2 * N:2 * N + E], x2T[s][:, c, :], w13s[:, c, HALF:HALF + E], start=(c == 0), stop=(c == 1))
                last.then_inc(logit_ps, 1)

            def rank(g, b):
                pe.wait_ge(picks, g + 1)
                mm(bank(b)[0:N, 0:GE], cst[0:N, C_TRI:C_TRI + N], rt[:, PICK, :], start=True, stop=True)
                mm(bank(b)[0:N, GE:2 * GE], cst[0:N, C_ONE:C_ONE + N], rt[:, PICK, :], start=True, stop=True)\
                    .then_inc(rank_ps, 1)

            def shared_in(n, s, half, up):
                width = HALF + (0 if up or half else E)
                for c in range(2):
                    at = up * (I + E) + half * (HALF + (0 if up else E))
                    last = mm(bank(4 + up)[0:N, 0:width], x2T[s][:, c, :], w13s[:, c, at:at + width],
                              start=(c == 0), stop=(c == 1))
                last.then_inc((g_ps, u_ps)[up], 1)

            def shared_turn(n, half):
                pe.wait_ge(hh_done, 2 * n + half + 1)
                if half == 0 and isinstance(n, int) and n == B - 1:
                    pe.wait_ge(logit_done, B)
                for k in range(KH):
                    last = nc.tensor.transpose(bank(6)[:, k * N:(k + 1) * N], hbuf[half][0:N, k * P:(k + 1) * P],
                                               ident[0:N, 0:N])
                last.then_inc(hT_ps, 1)

            def shared_down(n, half, parts=range(KH)):
                pe.wait_ge(hT_done, 2 * n + half + 1)
                if half == 0 and not (isinstance(n, int) and n == 0):
                    pe.wait_ge(sum_done, n)
                for k in parts:
                    kk = half * KH + k
                    last = mm(bank(7)[0:N, 0:D], hT[half][:, k, 0:N], wdns[:, kk * D:(kk + 1) * D],
                              start=(kk == 0), stop=(kk == I // P - 1))
                if half == 1 and k == KH - 1:
                    last.then_inc(y_ps, 1)

            def step(n, s, before, after, ranks, ranked):
                z = 1 - s
                if before:
                    transpose_x2(n - 1, z)
                scores(n, s, 0)
                if ranked is not None:
                    pe.wait_ge(rank_copied, ranked)
                values(n, s)
                if before:
                    pe.wait_ge(x2T_done, n)
                    shared_in(n - 1, z, 0, 0)
                scores(n, s, 1)
                transpose_p(n, s, 0)
                pe.wait_ge(v_done, n + 1)
                if before:
                    shared_in(n - 1, z, 0, 1)
                    pe.wait_ge(act_done, 2 * n - 1)
                    pe.wait_ge(gs_done, 2 * n - 1)
                weigh_v(n, s, 0, before)
                transpose_p(n, s, 1)
                if before:
                    shared_turn(n - 1, 0)
                    pe.wait_ge(clip_done, 2 * n - 1)
                weigh_v(n, s, 1, before, after)
                if after:
                    lora_down(n + 1, z)
                if before:
                    shared_down(n - 1, 0, range(KH - 1))
                transpose_o(n, s)
                if before:
                    shared_down(n - 1, 0, (KH - 1,))
                    shared_turn(n - 1, 1)
                project(n, s)
                if after:
                    transpose_hg(n + 1, z)
                if before:
                    shared_down(n - 1, 1, (0,))
                if after:
                    qk(n + 1, z)
                if before:
                    shared_down(n - 1, 1, range(1, KH))
                if ranks is not None:
                    rank(ranks, 5)

            pe.wait_ge(wa_in, 80)
            pe.wait_ge(ones_done, 6)
            pe.wait_ge(emb_done, ET)
            transpose_x(0, 0)
            lora_down(0, 0)
            transpose_hg(0, 0)
            qk(0, 0)
            step(0, 0, False, True, None, None)
            pe.wait_ge(w_shared, 64)
            step(1, 1, True, True, None, None)
            step(2, 0, True, True, None, None)
            step(3, 1, True, True, 0, None)
            with pe.Fori(2, B // 2 - 1) as i:
                step(2 * i, 0, True, True, None, i - 1)
                step(2 * i + 1, 1, True, True, i - 1, None)
            step(B - 2, 0, True, True, None, B // 2 - 2)
            step(B - 1, 1, True, False, None, None)
            transpose_x2(B - 1, 1)
            route(B - 1, 1)
            rank(B // 2 - 2, 5)
            shared_in(B - 1, 1, 0, 0)
            pe.wait_ge(rank_copied, B // 2 - 1)
            shared_in(B - 1, 1, 0, 1)
            rank(B // 2 - 1, 0)
            pe.wait_ge(act_done, 2 * B - 1)
            pe.wait_ge(gs_done, 2 * B - 1)
            shared_in(B - 1, 1, 1, 0)
            shared_turn(B - 1, 0)
            shared_in(B - 1, 1, 1, 1)
            shared_down(B - 1, 0)
            shared_turn(B - 1, 1)
            shared_down(B - 1, 1)

            def x_transpose(t, s, times):
                pe.wait_ge(x_in[s], times)
                for c in range(2):
                    last = nc.tensor.transpose(ps[0:DC, 7, c * P:(c + 1) * P], xin[s][:, c * DC:(c + 1) * DC], ident)
                last.then_inc(rxT_ps, 1)

            def gate_up(e, s, half, up):
                for c in range(2):
                    at = c * 2 * I + up * I + half * HALF
                    last = mm(ps[:, 2 * up + half, 0:HALF], xT[s][:, c, :], w13[0:DC, e, at:at + HALF],
                              start=(c == 0), stop=(c == 1))
                last.then_inc((rg_ps, ru_ps)[up], 1)

            def h_transpose(t, half):
                pe.wait_ge(rhh_done, 2 * t + half + 1)
                for k in range(KH):
                    last = nc.tensor.transpose(ps[:, 4 + half, k * P:(k + 1) * P], hbuf[half][:, k * P:(k + 1) * P], ident)
                last.then_inc(rhT_ps, 1)

            def down(t, e, half):
                pe.wait_ge(rhT_done, 2 * t + half + 1)
                if half == 0 and not (isinstance(t, int) and t == 0):
                    pe.wait_ge(y_done, t)
                for k in range(KH):
                    kk = half * KH + k
                    last = mm(ps[:, 6, 0:D], hT[half][:, k, :], wdn[:, e, kk * D:(kk + 1) * D],
                              start=(kk == 0), stop=(kk == I // P - 1))
                if half == 1:
                    last.then_inc(ry_ps, 1)

            def tile(t, s, e, e_before, times):
                pe.wait_ge(rxT_done, t + 1)
                gate_up(e, s, 0, 0)
                h_transpose(t - 1, 1)
                gate_up(e, s, 0, 1)
                down(t - 1, e_before, 1)
                x_transpose(t + 1, 1 - s, times)
                gate_up(e, s, 1, 0)
                h_transpose(t, 0)
                gate_up(e, s, 1, 1)
                down(t, e, 0)

            def experts(t, n):
                _, e = nc.values_load_multi_w_load_instructions(
                    etab[0:1, bass.ds(t, n)], engines=(mybir.EngineType.PE,), min_val=0, max_val=E - 1,
                    skip_runtime_bounds_check_because="the router writes 0 to E - 1")
                return e

            pe.wait_ge(sum_done, B)
            x_transpose(0, 0, 16)
            e0, = experts(0, 1)
            pe.wait_ge(rxT_done, 1)
            gate_up(e0, 0, 0, 0)
            gate_up(e0, 0, 0, 1)
            x_transpose(1, 1, 16)
            gate_up(e0, 0, 1, 0)
            h_transpose(0, 0)
            gate_up(e0, 0, 1, 1)
            down(0, e0, 0)
            with pe.Fori(0, (TILES - 1) // 2) as i:
                ea, eb, ec = experts(2 * i, 3)
                tile(2 * i + 1, 1, eb, ea, 16 * i + 32)
                tile(2 * i + 2, 0, ec, eb, 16 * i + 32)
            ea, eb = experts(TILES - 2, 2)
            tile(TILES - 1, 1, eb, ea, 8 * (LOADS + 1))
            h_transpose(TILES - 1, 1)
            down(TILES - 1, eb, 1)

        @block.scalar
        def _(act):
            cp = nc.scalar.copy
            act.wait_ge(const_in, 80)
            act.wait_ge(wa_in, 80)
            for src, at, w in ((w1s[:, 0:HALF], 0, HALF), (w1s[:, HALF:], HALF + E, HALF), (w3s, I + E, I)):
                act.dma_start(w13s[:, :, at:at + w], src.rearrange("(c p) i -> p c i", c=2)).then_inc(w_shared, 16)
            act.dma_start(wdns[:, :].rearrange("p (k d) -> p k d", d=D),
                          w2s.rearrange("(k p) d -> p k d", p=P)).then_inc(w_shared, 16)

            def x_copies(n, s):
                act.wait_ge(xT_ps, n + 1)
                cp(xT1[s][:, 0, :], bank(2)[:, 0:N]).then_inc(xT_done, 1)
                cp(xT1[s][0:PP, 1, :], bank(2)[0:PP, N:2 * N]).then_inc(xT_done, 1)

            def gate_exp(n, s):
                act.wait_ge(gmax, n + 1)
                nc.scalar.activation(st[s][:, 20:20 + E], bank(2)[0:N, 2 * N + E * R:2 * N + NLG], ACT.Exp,
                                     bias=st[s][:, 16:17], accum_out=st[s][:, 17:18]).then_inc(gexp, 1)

            def hg_copy(n, s):
                act.wait_ge(hgT_ps, n + 1)
                cp(xT1[s][:, 1, :], bank(2)[:, 0:N]).then_inc(hgT_done, 1)

            def p_exp(n, s, half):
                act.wait_ge(ssub, 2 * n + half + 1)
                part = prob[s][:, half * 6 * N:(half + 1) * 6 * N]
                nc.scalar.activation(part, part, ACT.Exp, scale=SCALE).then_inc(p_done, 1)

            def pT_copy(n, s, half):
                act.wait_ge(pT_ps, 2 * n + half + 1)
                cp(probT[s][:, half * 6 * N:(half + 1) * 6 * N].rearrange("p (b m) -> p b m", b=2),
                   ps[0:N, 2 * half:2 * half + 2, 0:3 * N]).then_inc(pT_done, 1)

            def oT_copy(n, s):
                act.wait_ge(oT_ps, n + 1)
                cp(oT[s][0:DC, :, :].rearrange("p c n -> p (c n)"), bank(1)[0:DC, 0:2 * N]).then_inc(oT_done, 1)

            def x2T_copy(n, s):
                act.wait_ge(x2T_ps, n + 1)
                cp(x2T[s][:, :, :].rearrange("p c n -> p (c n)"), bank(6)[0:DC, 0:2 * N]).then_inc(x2T_done, 1)

            def shared_tanh(n, half):
                act.wait_ge(g_ps, 2 * n + half + 1)
                nc.scalar.activation(gbuf[half][0:N, :], bank(4)[0:N, 0:HALF], ACT.Tanh, scale=0.5).then_inc(act_done, 1)

            def shared_turned(n, half):
                act.wait_ge(hT_ps, 2 * n + half + 1)
                nc.scalar.activation(hT[half][:, :, 0:N], bank(6)[:, 0:KH * N].rearrange("p (k n) -> p k n", k=KH),
                                     ACT.Copy, scale=0.5).then_inc(hT_done, 1)

            def group_exp(g):
                act.wait_ge(absl, g + 1)
                nc.scalar.activation(rt[:, U, :], rt[:, TMP, :], ACT.Exp, scale=-1.0).then_inc(uexp, 1)

            def step(n, s, before, after, group):
                z = 1 - s
                if before:
                    x2T_copy(n - 1, z)
                p_exp(n, s, 0)
                if before:
                    shared_tanh(n - 1, 0)
                pT_copy(n, s, 0)
                p_exp(n, s, 1)
                if group is not None:
                    group_exp(group)
                pT_copy(n, s, 1)
                if before:
                    shared_turned(n - 1, 0)
                    shared_tanh(n - 1, 1)
                if after:
                    x_copies(n + 1, z)
                oT_copy(n, s)
                if after:
                    gate_exp(n + 1, z)
                if before:
                    shared_turned(n - 1, 1)
                if after:
                    hg_copy(n + 1, z)

            x_copies(0, 0)
            gate_exp(0, 0)
            hg_copy(0, 0)
            with act.Fori(0, E - LATE) as e:
                load_expert(act, w1, w2, w3, w13, wdn, w_in, e)
            step(0, 0, False, True, None)
            step(1, 1, True, True, None)
            step(2, 0, True, True, 0)
            step(3, 1, True, True, None)
            with act.Fori(2, B // 2 - 1) as i:
                step(2 * i, 0, True, True, i - 1)
                step(2 * i + 1, 1, True, True, None)
            step(B - 2, 0, True, True, B // 2 - 2)
            step(B - 1, 1, True, False, None)
            x2T_copy(B - 1, 1)
            group_exp(B // 2 - 1)
            shared_tanh(B - 1, 0)
            act.wait_ge(row_done, B)
            act.wait_ge(scat1, 16 * (B - 2 * GB))
            act.wait_ge(scat2, 16 * (B - 2 * GB))
            for g in range(2):
                for k in range(GB):
                    for c in range(2):
                        cp(last_rows[g][k][c][:, 0:WT], rows[:, B - 2 * GB + GB * g + k, 0:WT]).then_inc(staged, 1)
            shared_tanh(B - 1, 1)
            shared_turned(B - 1, 0)
            shared_turned(B - 1, 1)
            nc.scalar.activation(st[0][0:1, 30:31], cst[0:1, 0:1], ACT.Silu)
            act.wait_ge(sum_done, B)
            act.dma_start(acc[(B - 1) * N:T, :], h2[1][:, :]).then_inc(acc_out[1], 16)

            def silu(t, half):
                act.wait_ge(rg_ps, 2 * t + half + 1)
                nc.scalar.activation(gbuf[half][:, :], ps[:, half, 0:HALF], ACT.Silu).then_inc(silu_done, 1)

            def hT_copy(t, half):
                act.wait_ge(rhT_ps, 2 * t + half + 1)
                cp(hT[half][:, :, :].rearrange("p k n -> p (k n)"), ps[:, 4 + half, 0:HALF]).then_inc(rhT_done, 1)

            def xT_copy(t, s):
                act.wait_ge(rxT_ps, t + 1)
                cp(xT[s][:, :, :].rearrange("p c n -> p (c n)"), ps[0:DC, 7, 0:2 * P]).then_inc(rxT_done, 1)

            def tile(t, s):
                silu(t, 0)
                hT_copy(t - 1, 1)
                xT_copy(t + 1, 1 - s)
                silu(t, 1)
                hT_copy(t, 0)

            xT_copy(0, 0)
            silu(0, 0)
            xT_copy(1, 1)
            silu(0, 1)
            hT_copy(0, 0)
            with act.Fori(0, (TILES - 1) // 2) as i:
                tile(2 * i + 1, 1)
                tile(2 * i + 2, 0)
            tile(TILES - 1, 1)
            hT_copy(TILES - 1, 1)

        @block.gpsimd
        def _(pool):
            pool.wait_ge(const_in, 80)

            def rstd_of(n, s, mv, at, done, count):
                pool.wait_ge(mv, n + 1)
                pool.tensor_tensor(st[s][:, at:at + 1], st[s][:, at - 1:at], cst[0:N, C_POW + 2:C_POW + 3],
                                   ALU.add).then_inc(veps, 1)
                pool.wait_ge(veps, count)
                pool.tensor_tensor(st[s][:, at + 1:at + 2], st[s][:, at:at + 1], cst[0:N, C_POW:C_POW + 1],
                                   ALU.pow).then_inc(done, 1)

            def scatter(g, k):
                pool.wait_ge(weights, g + 1)
                pool.wait_ge(slots, g + 1)
                pool.wait_ge(row_done, 2 * g + k + 1)
                n = 2 * g + k
                for c, (row, slot, done) in enumerate(((row1, slots_of[0][0], scat1), (row2, slots_of[0][1], scat2))):
                    pool.nop(nofuse=True)
                    pool.tensor_copy(row[k][:, 0:WT], rows[:, bass.ds(n, 1), 0:WT].rearrange("p a c -> p (a c)"))\
                        .then_inc(copied, 1)
                    pool.tensor_copy(row[k][:, WT:WT + 1], rs[:, 2 + c, k:k + 1]).then_inc(weighted, 1)
                    pool.wait_ge(copied, 4 * g + 2 * k + c + 1)
                    pool.wait_ge(weighted, 4 * g + 2 * k + c + 1)
                    pool.nop(nofuse=True)
                    pool.indirect_dma_start(xs[:, :], bass.IndirectOffsetOnAxis(slot[:, k:k + 1], 0),
                                            row[k][:, :], None).then_inc(done, 16)

            def square_root(g):
                pool.wait_ge(softp, g + 1)
                pool.tensor_tensor(rt[:, SC, :], rt[:, SP, :], cst[0:N, C_POW + 1:C_POW + 2].broadcast_to([N, GE]),
                                   ALU.pow).then_inc(root, 1)

            def step(n, s, after, out, group):
                if after:
                    rstd_of(n + 1, 1 - s, mv1, 8, rstd1, 2 * n + 2)
                if out is not None:
                    scatter(out, s)
                rstd_of(n, s, mv2, 12, rstd2, 2 * n + 3 if after else 2 * n + 2)
                pool.wait_ge(x2_done, n + 1)
                pool.nop(nofuse=True)
                pool.tensor_copy(rows[:, bass.ds(n, 1), 0:D], x2[s][:, :].unsqueeze(1)).then_inc(row_done, 1)
                if group is not None:
                    square_root(group)

            rstd_of(0, 0, mv1, 8, rstd1, 1)
            step(0, 0, True, None, None)
            step(1, 1, True, None, None)
            step(2, 0, True, None, 0)
            step(3, 1, True, None, None)
            step(4, 0, True, 0, 1)
            step(5, 1, True, 0, None)
            with pool.Fori(3, B // 2 - 1) as i:
                step(2 * i, 0, True, i - 2, i - 1)
                step(2 * i + 1, 1, True, i - 2, None)
            step(B - 2, 0, True, B // 2 - 3, B // 2 - 2)
            step(B - 1, 1, False, B // 2 - 3, None)
            last = B // 2 - 1
            square_root(last)
            pool.wait_ge(fill_out, 16 * E)
            for g in (last - 1, last):
                pool.wait_ge(slots, g + 1)
                pool.wait_ge(weights, g + 1)
                for k in range(GB):
                    for c, done in enumerate((scat1, scat2)):
                        row = last_rows[g - last + 1][k][c]
                        pool.wait_ge(staged, 4 * (g - last + 1) + 2 * k + c + 1)
                        pool.tensor_copy(row[:, WT:WT + 1], rs[:, 2 + c, k:k + 1]).then_inc(weighted, 1)
                        pool.wait_ge(weighted, 4 * g + 2 * k + c + 1)
                        pool.indirect_dma_start(xs[:, :], bass.IndirectOffsetOnAxis(slots_of[g - last + 1][c][:, k:k + 1], 0),
                                                row[:, 0:ROW], None).then_inc(done, 16)

            def add_rows(t, s):
                pool.wait_ge(meta_done, t + 1)
                pool.nop(nofuse=True)
                pool.tensor_copy(idx[s][:, :], meta[:, bass.ds(t, 1), 0]).then_inc(idx_done, 1)
                pool.wait_ge(idx_done, t + 1)
                pool.wait_ge(y_done, t + 1)
                if not (isinstance(t, int) and t == 0):
                    pool.wait_ge(y_out, 16 * t)
                pool.nop(nofuse=True)
                pool.indirect_dma_start(acc[:, :], bass.IndirectOffsetOnAxis(idx[s][:, 0:1], 0),
                                        yout[s][:, :], None, compute_op=ALU.add).then_inc(y_out, 16)

            pool.wait_ge(spare_out, 32)
            pool.wait_ge(acc_out[0], 8 * B)
            pool.wait_ge(acc_out[1], 8 * B)
            add_rows(0, 0)
            with pool.Fori(0, (TILES - 1) // 2) as i:
                add_rows(2 * i + 1, 1)
                add_rows(2 * i + 2, 0)
            add_rows(TILES - 1, 1)

        @block.vector
        def _(dve):
            V = nc.vector
            V.memset(filler[:, 0:D], 0.0).then_inc(fill_done, 1)
            V.memset(filler[:, WT:WT + 1], 0.0).then_inc(fill_done, 1)
            for s in range(2):
                V.memset(oT[s][DC:DC + 1, 1, :], 1.0).then_inc(ones_done, 1)
                V.memset(va[s][:, :, HD:VW], 1.0).then_inc(ones_done, 1)
            dve.wait_ge(const_in, 80)
            V.tensor_copy(filler[:, ID:ID + 1], cst[:, C_FILL:C_FILL + 1]).then_inc(fill_done, 1)
            V.tensor_copy(rows[:, :, ID], cst[0:N, C_TOK:C_TOK + B]).then_inc(ones_done, 1)
            V.tensor_copy(run[:, :], cst[0:N, C_REG:C_REG + E]).then_inc(ones_done, 1)
            V.tensor_tensor(clsrow, clsrow, small_sb[:, 2 * D:3 * D], ALU.add).then_inc(cls_done, 1)
            def norm1(n, s, times):
                dve.wait_ge(h_in[s], times)
                V.bn_stats(st[s][:, 0:6], h[s][:, :]).then_inc(bn1, 1)
                dve.wait_ge(bn1, n + 1)
                dve.nop(nofuse=True)
                V.bn_aggr(st[s][:, 6:8], st[s][:, 0:6]).then_inc(mv1, 1)

            def norm1_end(n, s):
                dve.wait_ge(rstd1, n + 1)
                V.tensor_scalar(xh[s][:, 0:D], h[s][:, :], st[s][:, 6:7], st[s][:, 9:10], ALU.subtract, ALU.mult)\
                    .then_inc(xn_done, 1)

            def gate_max(n, s):
                dve.wait_ge(lora_ps, n + 1)
                V.tensor_reduce(st[s][:, 16:17], bank(2)[0:N, 2 * N + E * R:2 * N + NLG], AX.X, ALU.max, negate=True)\
                    .then_inc(gmax, 1)

            def gated(n, s):
                dve.wait_ge(gexp, n + 1)
                V.reciprocal(st[s][:, 18:19], st[s][:, 17:18]).then_inc(grcp, 1)
                dve.wait_ge(grcp, n + 1)
                V.scalar_tensor_tensor(xh[s][:, D:2 * P].rearrange("p (e r) -> p e r", r=R),
                                       bank(2)[0:N, 2 * N:2 * N + E * R].rearrange("p (e r) -> p e r", r=R), st[s][:, 18:19],
                                       st[s][:, 20:20 + E].unsqueeze(2).broadcast_to([N, E, R]),
                                       ALU.mult, ALU.mult).then_inc(hg_done, 1)

            def qk_bias(n, s, b):
                dst, done_ps, done = ((qT, q_ps, q_done), (kT, k_ps, k_done))[b - 1]
                dve.wait_ge(done_ps, n + 1)
                V.tensor_tensor(dst[s].rearrange("p (g m) -> p g m", g=NG),
                                bank(b)[:, 0:NG * N].rearrange("p (g m) -> p g m", g=NG),
                                bqk_sb[:, (b - 1) * NG:b * NG].unsqueeze(2).broadcast_to([P, NG, N]),
                                ALU.add).then_inc(done, 1)

            def v_bias(n, s):
                dve.wait_ge(v_ps, n + 1)
                V.tensor_tensor(va[s][:, :, 0:HD], bank(5)[0:N, 2 * GE:2 * GE + D].rearrange("p (h d) -> p h d", d=HD),
                                bv_sb[:, :].rearrange("p (h d) -> p h d", d=HD), ALU.add).then_inc(v_done, 1)

            def softmax(n, s, half):
                dve.wait_ge(s_ps, 2 * n + half + 1)
                sv = ps[0:N, 2 * half:2 * half + 2, 0:NG * N].rearrange("p j (g k) -> p j g k", g=NG)
                mx = smx[s][:, 6 * half:6 * half + 6].rearrange("p (j g) -> p j g", j=2)
                V.tensor_reduce(mx, sv, AX.X, ALU.max).then_inc(smax, 1)
                dve.wait_ge(smax, 2 * n + half + 1)
                V.tensor_tensor(prob[s][:, half * 6 * N:(half + 1) * 6 * N].rearrange("p (j g k) -> p j g k", j=2, g=NG),
                                sv, mx.unsqueeze(3).broadcast_to([N, 2, NG, N]), ALU.subtract).then_inc(ssub, 1)

            def attend_end(n, s):
                dve.wait_ge(pv_ps, n + 1)
                ov = bank(0)[0:N, 0:H * VW].rearrange("p (h d) -> p h d", d=VW)
                V.reciprocal(smx[s][:, H:2 * H], ov[:, :, HD]).then_inc(ssum, 1)
                dve.wait_ge(ssum, n + 1)
                V.tensor_tensor(o[s][:, :].rearrange("p (h d) -> p h d", d=HD), ov[:, :, 0:HD],
                                smx[s][:, H:2 * H].unsqueeze(2).broadcast_to([N, H, HD]), ALU.mult).then_inc(o_done, 1)

            def residual(n, s, times):
                if times is not None:
                    dve.wait_ge(acc_out[s], times)
                dve.wait_ge(proj_ps, n + 1)
                V.tensor_tensor(h2[s][:, :], bank(3)[0:N, 0:D], h[s][:, :], ALU.add).then_inc(h2_done, 1)
                dve.wait_ge(h2_done, n + 1)
                V.bn_stats(st[s][:, 0:6], h2[s][:, :]).then_inc(bn2, 1)
                dve.wait_ge(bn2, n + 1)
                dve.nop(nofuse=True)
                V.bn_aggr(st[s][:, 10:12], st[s][:, 0:6]).then_inc(mv2, 1)

            def norm2(n, s):
                dve.wait_ge(rstd2, n + 1)
                V.tensor_scalar(x2[s][:, :], h2[s][:, :], st[s][:, 10:11], st[s][:, 13:14], ALU.subtract, ALU.mult)\
                    .then_inc(x2_done, 1)

            def logit_copy(n, s, logits):
                V.tensor_copy(rt[:, LG, s * E:(s + 1) * E], logits).then_inc(logit_done, 1)

            def shared_gate(n, half):
                dve.wait_ge(act_done, 2 * n + half + 1)
                V.scalar_tensor_tensor(gbuf[half][0:N, :], gbuf[half][0:N, :], 1.0, bank(4)[0:N, 0:HALF],
                                       ALU.add, ALU.mult).then_inc(gs_done, 1)

            def shared_clip(n, half):
                dve.wait_ge(u_ps, 2 * n + half + 1)
                V.tensor_scalar(ubuf[half][0:N, :], bank(5)[0:N, 0:HALF], -LIMIT, LIMIT, ALU.max, ALU.min)\
                    .then_inc(clip_done, 1)

            def shared_product(n, half):
                dve.wait_ge(gs_done, 2 * n + half + 1)
                dve.wait_ge(clip_done, 2 * n + half + 1)
                V.scalar_tensor_tensor(hbuf[half][0:N, :], gbuf[half][0:N, :], 2 * SILU_LIMIT, ubuf[half][0:N, :],
                                       ALU.min, ALU.mult).then_inc(hh_done, 1)

            def shared_sum(n, s):
                dve.wait_ge(y_ps, n + 1)
                dve.wait_ge(x2_done, n + 1)
                V.tensor_tensor(h2[s][:, :], bank(7)[0:N, 0:D], h2[s][:, :], ALU.add).then_inc(sum_done, 1)

            steps, linked = [0], [None]

            def link(g, ins):
                steps[0] += 1
                ins.then_inc(rstep, 1)
                dve.wait_ge(rstep, RSTEPS * (g if linked[0] is None else linked[0]) + steps[0])

            def rv(k):
                return rt[:, k, :].rearrange("p (n e) -> p n e", e=E)

            def over_e(a):
                return a.unsqueeze(2).broadcast_to([N, GB, E])

            iota = cst[0:N, C_IOTA:C_IOTA + GE]

            def absolute(g):
                V.scalar_tensor_tensor(rt[:, TMP, :], rt[:, LG, :], -1.0, rt[:, LG, :], ALU.mult, ALU.max).then_inc(absl, 1)

            def softplus_a(g):
                dve.wait_ge(uexp, g + 1)
                link(g, V.tensor_scalar(rt[:, Z, :], rt[:, U, :], 2.0, None, ALU.add))
                link(g, V.reciprocal(rt[:, Z, :], rt[:, Z, :]))
                link(g, V.tensor_tensor(rt[:, Z, :], rt[:, Z, :], rt[:, U, :], ALU.mult))

            def series(g, odds):
                for c in odds:
                    link(g, V.scalar_tensor_tensor(rt[:, Q, :], rt[:, Q, :], 1.0 / c, rt[:, Z2, :], ALU.add, ALU.mult))

            def softplus_b(g):
                link(g, V.tensor_tensor(rt[:, Z2, :], rt[:, Z, :], rt[:, Z, :], ALU.mult))
                link(g, V.tensor_scalar(rt[:, Q, :], rt[:, Z2, :], 1.0 / 17, 1.0 / 15, ALU.mult, ALU.add))
                link(g, V.tensor_tensor(rt[:, Q, :], rt[:, Q, :], rt[:, Z2, :], ALU.mult))
                series(g, (13, 11, 9))

            def softplus_c(g):
                series(g, (7, 5, 3))
                link(g, V.scalar_tensor_tensor(rt[:, Q, :], rt[:, Q, :], 1.0, rt[:, Z, :], ALU.add, ALU.mult))
                link(g, V.tensor_scalar(rt[:, Z, :], rt[:, LG, :], 0.0, None, ALU.max))
                V.scalar_tensor_tensor(rt[:, SP, :], rt[:, Q, :], 2.0, rt[:, Z, :], ALU.mult, ALU.add).then_inc(softp, 1)

            def choose(g, mask, col):
                link(g, V.tensor_reduce(rs[:, col, :], rv(A), AX.X, ALU.max))
                link(g, V.tensor_tensor(rv(mask), rv(A), over_e(rs[:, col, :]), ALU.is_ge))
                link(g, V.tensor_tensor(rt[:, mask, :], rt[:, mask, :], iota, ALU.mult))
                link(g, V.tensor_reduce(rs[:, col, :], rv(mask), AX.X, ALU.min))
                link(g, V.tensor_tensor(rv(mask), iota.rearrange("p (n e) -> p n e", e=E), over_e(rs[:, col, :]), ALU.is_equal))

            def first_choice(g):
                dve.wait_ge(root, g + 1)
                link(g, V.tensor_tensor(rt[:, A, :], rt[:, SC, :], cst[0:N, C_BIAS:C_BIAS + GE], ALU.add))
                choose(g, M1, 0)
                link(g, V.scalar_tensor_tensor(rt[:, A, :], rt[:, M1, :], -3.0e38, rt[:, A, :], ALU.mult, ALU.add))

            def second_choice(g):
                choose(g, M2, 1)
                V.tensor_tensor(rt[:, PICK, :], rt[:, M1, :], rt[:, M2, :], ALU.add).then_inc(picks, 1)

            def shares(g):
                if not (isinstance(g, int) and g == 0):
                    dve.wait_ge(weighted, 4 * g)
                link(g, V.tensor_tensor(rt[:, W0, :], rt[:, M1, :], rt[:, SC, :], ALU.mult))
                link(g, V.tensor_tensor(rt[:, W1, :], rt[:, M2, :], rt[:, SC, :], ALU.mult))
                link(g, V.tensor_reduce(rs[:, 2:4, :], rt[:, W0:W0 + 2, :].rearrange("p a (n e) -> p a n e", e=E), AX.X, ALU.add))
                link(g, V.tensor_tensor(rs[:, 4, :], rs[:, 2, :], rs[:, 3, :], ALU.add))
                link(g, V.tensor_scalar(rs[:, 4, :], rs[:, 4, :], 1e-6, None, ALU.max))
                link(g, V.reciprocal(rs[:, 4, :], rs[:, 4, :]))
                V.tensor_tensor(rs[:, 2:4, :], rs[:, 2:4, :], rs[:, 4, :].unsqueeze(1).broadcast_to([N, 2, GB]), ALU.mult)\
                    .then_inc(weights, 1)

            def rank_copy(g, b):
                dve.wait_ge(rank_ps, g + 1)
                V.tensor_copy(rt[:, W2:W2 + 2, :].rearrange("p a b -> p (a b)"), bank(b)[0:N, 0:2 * GE]).then_inc(rank_copied, 1)

            def place_rows(g, slot1=slots_of[0][0], slot2=slots_of[0][1], reused=True):
                dve.wait_ge(rank_copied, g + 1)
                if reused and not (isinstance(g, int) and g == 0):
                    dve.wait_ge(scat2, 32 * g)
                    dve.wait_ge(scat1, 32 * g)
                for k in range(GB):
                    part = slice(k * E, (k + 1) * E)
                    link(g, V.tensor_tensor(rt[:, RANK, part], rt[:, W2, part], run[:, :], ALU.add))
                    link(g, V.tensor_tensor(run[:, :], run[:, :], rt[:, W3, part], ALU.add))
                link(g, V.tensor_tensor(rt[:, W0, :], rt[:, M1, :], rt[:, RANK, :], ALU.mult))
                link(g, V.tensor_tensor(rt[:, W1, :], rt[:, M2, :], rt[:, RANK, :], ALU.mult))
                link(g, V.tensor_reduce(rs[:, 6:8, :], rt[:, W0:W0 + 2, :].rearrange("p a (n e) -> p a n e", e=E), AX.X, ALU.add))
                V.tensor_copy(slot1[:, :], rs[:, 6, :])
                V.tensor_copy(slot2[:, :], rs[:, 7, :]).then_inc(slots, 1)

            def step(n, s, before, after, times, stored, place, soft, pick):
                z = 1 - s
                if place is not None:
                    rank_copy(place, 5)
                softmax(n, s, 0)
                v_bias(n, s)
                if place is not None:
                    steps[0] = PLACED
                    shares(place)
                if pick is not None:
                    softplus_c(pick)
                if before:
                    dve.wait_ge(act_done, 2 * n - 1)
                    dve.nop(nofuse=True)
                    logit_copy(n - 1, z, bank(4)[0:N, HALF:HALF + E])
                    if soft is not None:
                        dve.wait_ge(logit_done, n)
                        absolute(soft)
                    shared_gate(n - 1, 0)
                softmax(n, s, 1)
                if after:
                    norm1(n + 1, z, times)
                if before:
                    shared_clip(n - 1, 0)
                    shared_product(n - 1, 0)
                if after:
                    norm1_end(n + 1, z)
                if place is not None:
                    place_rows(place)
                    if isinstance(place, int) and place == B // 2 - 3:
                        V.tensor_copy(ftab[:, :], run[0:1, :]).then_inc(fill_from, 1)
                if pick is not None:
                    first_choice(pick)
                if before:
                    shared_gate(n - 1, 1)
                    shared_clip(n - 1, 1)
                attend_end(n, s)
                if before:
                    shared_product(n - 1, 1)
                if after:
                    gate_max(n + 1, z)
                if soft is not None:
                    steps[0] = 0
                    softplus_a(soft)
                if after:
                    gated(n + 1, z)
                residual(n, s, stored)
                if soft is not None:
                    softplus_b(soft)
                if pick is not None:
                    second_choice(pick)
                if after:
                    qk_bias(n + 1, z, 1)
                norm2(n, s)
                if after:
                    qk_bias(n + 1, z, 2)
                if before:
                    shared_sum(n - 1, z)

            for t in range(ET):
                if t == ET - 1:
                    norm1(0, 0, 48)
                w = min(P, B * NPATCH - t * P)
                dve.wait_ge(emb_ps, t + 1)
                V.tensor_tensor(emb_sb[0:w, t, :], bank(t)[0:w, 0:D], pr_sb[0:w, t, :], ALU.add).then_inc(emb_done, 1)
            norm1_end(0, 0)
            gate_max(0, 0)
            gated(0, 0)
            qk_bias(0, 0, 1)
            qk_bias(0, 0, 2)
            step(0, 0, False, True, 48, None, None, None, None)
            step(1, 1, True, True, 96, None, None, None, None)
            step(2, 0, True, True, 96, 16, None, 0, None)
            step(3, 1, True, True, 144, 16, None, None, 0)
            step(4, 0, True, True, 144, 32, 0, 1, None)
            step(5, 1, True, True, 192, 32, None, None, 1)
            with dve.Fori(3, B // 2 - 1) as i:
                step(2 * i, 0, True, True, 48 * i + 48, 16 * i, i - 2, i - 1, None)
                step(2 * i + 1, 1, True, True, 48 * i + 96, 16 * i, None, None, i - 1)
            last = B // 2 - 1
            step(B - 2, 0, True, True, 48 * last + 48, 16 * last, last - 2, last - 1, None)
            step(B - 1, 1, True, False, None, 16 * last, None, None, last - 1)

            steps[0], linked[0] = PLACED, last - 1
            shares(last - 1)
            dve.wait_ge(logit_ps, 1)
            logit_copy(B - 1, 1, bank(6)[0:N, 2 * N:2 * N + E])
            dve.wait_ge(logit_done, B)
            absolute(last)
            rank_copy(last - 1, 5)
            softplus_a(last)
            softplus_b(last)
            softplus_c(last)
            place_rows(last - 1)
            shared_gate(B - 1, 0)
            shared_clip(B - 1, 0)
            shared_product(B - 1, 0)
            first_choice(last)
            second_choice(last)
            rank_copy(last, 0)
            place_rows(last, *slots_of[1], reused=False)
            shares(last)
            assert steps[0] == 2 * RSTEPS

            ends = [0]

            def then(ins):
                ends[0] += 1
                ins.then_inc(rstep, 1)
                dve.wait_ge(rstep, RSTEPS * (B // 2) + ends[0])

            then(V.tensor_tensor(off[:, 5, :], run[:, :], cst[0:N, C_REG:C_REG + E], ALU.subtract))
            jc = jcmp[:, 0:E * MOST].rearrange("p (e j) -> p e j", e=E)
            then(V.tensor_tensor(jc, off[:, 5, :].unsqueeze(2).broadcast_to([N, E, MOST]),
                                 cst[0:N, C_J:C_J + E * MOST].rearrange("p (e j) -> p e j", e=E), ALU.is_gt))
            then(V.tensor_reduce(off[:, 0, :], jc, AX.X, ALU.add))
            for k, sh in enumerate((1, 2, 4)):
                then(V.tensor_copy(off[:, k + 1, 0:sh], off[:, k, 0:sh]))
                then(V.tensor_tensor(off[:, k + 1, sh:], off[:, k, sh:], off[:, k, 0:E - sh], ALU.add))
            te = jcmp[:, 0:LOADS * E].rearrange("p (t e) -> p t e", e=E)
            then(V.tensor_tensor(te, cst[0:N, C_T:C_T + LOADS * E].rearrange("p (t e) -> p t e", e=E),
                                 off[:, 3, :].unsqueeze(1).broadcast_to([N, LOADS, E]), ALU.is_ge))
            then(V.tensor_reduce(tv[:, 0, :], te, AX.X, ALU.add))
            then(V.tensor_tensor(te, te, off[:, 0, :].unsqueeze(1).broadcast_to([N, LOADS, E]), ALU.mult))
            then(V.tensor_reduce(tv[:, 1, :], te, AX.X, ALU.add))
            then(V.tensor_tensor(tv[:, 1, :], cst[0:N, C_TT:C_TT + LOADS], tv[:, 1, :], ALU.subtract))
            then(V.tensor_scalar(tv[:, 1, :], tv[:, 1, :], float(P), None, ALU.mult))
            then(V.scalar_tensor_tensor(tv[:, 1, :], tv[:, 0, :], float(REGION), tv[:, 1, :], ALU.mult, ALU.add))
            then(V.tensor_copy(rtab[:, :], tv[0:1, 1, :]))
            then(V.tensor_scalar(tv[:, 1, :], tv[:, 0, :], float(E - 1), None, ALU.min))
            then(V.tensor_copy(etab[:, 0:LOADS], tv[0:1, 1, :]))
            then(V.tensor_scalar(tv[:, 2, :], tv[:, 0, :], float(E - LATE), None, ALU.is_ge))
            then(V.tensor_scalar(tv[:, 2, :], tv[:, 2, :], 48.0 * LATE, 48.0 * (E - LATE), ALU.mult, ALU.add))
            V.tensor_copy(wtab[:, :], tv[0:1, 2, :]).then_inc(tables, 1)

            shared_gate(B - 1, 1)
            shared_clip(B - 1, 1)
            shared_product(B - 1, 1)
            shared_sum(B - 1, 1)

            def hidden(t, half):
                dve.wait_ge(ru_ps, 2 * t + half + 1)
                V.tensor_scalar(ubuf[half][:, :], ps[:, 2 + half, 0:HALF], -LIMIT, LIMIT, ALU.max, ALU.min)\
                    .then_inc(rclip_done, 1)
                dve.wait_ge(rclip_done, 2 * t + half + 1)
                dve.wait_ge(silu_done, 2 * t + half + 1)
                V.scalar_tensor_tensor(hbuf[half][:, :], gbuf[half][:, :], SILU_LIMIT, ubuf[half][:, :],
                                       ALU.min, ALU.mult).then_inc(rhh_done, 1)

            def meta_copy(t, s, times):
                dve.wait_ge(x_in[s], times)
                V.tensor_copy(meta[:, bass.ds(t, 1), :], xin[s][:, ID:ROW].unsqueeze(1)).then_inc(meta_done, 1)

            def result(t, s):
                dve.wait_ge(ry_ps, t + 1)
                if not (isinstance(t, int) and t < 2):
                    dve.wait_ge(y_out, 16 * t - 16)
                V.tensor_scalar(yout[s][:, :], ps[:, 6, 0:D], meta[:, bass.ds(t, 1), 1], None, ALU.mult)\
                    .then_inc(y_done, 1)

            meta_copy(0, 0, 16)
            hidden(0, 0)
            meta_copy(1, 1, 16)
            hidden(0, 1)

            def tile(t, s, times):
                hidden(t, 0)
                meta_copy(t + 1, 1 - s, times)
                result(t - 1, 1 - s)
                hidden(t, 1)

            tile(1, 1, 32)
            tile(2, 0, 32)
            with dve.Fori(1, (TILES - 1) // 2) as i:
                tile(2 * i + 1, 1, 16 * i + 32)
                tile(2 * i + 2, 0, 16 * i + 32)
            tile(TILES - 1, 1, 8 * (LOADS + 1))
            result(TILES - 1, 1)


SOFT = 14
PLACED = SOFT + 7 + 5
RSTEPS = PLACED + 6 + 7


def kernel(**inputs):
    import numpy as np
    import concourse.bacc as bacc
    from concourse import mybir as _mybir
    from concourse.bass_utils import run_bass_kernel_spmd as run

    a = {k: np.asarray(v) for k, v in inputs.items()}
    f32 = np.float32

    x = a["x"].reshape(B, 3, 6, 16, 6, 16).transpose(1, 3, 5, 0, 2, 4).reshape(6, P, B * NPATCH)
    patches = x.transpose(1, 0, 2)
    proj_w = a["L0_tok_proj_w"].T.reshape(6, P, D).transpose(1, 0, 2)
    pos = a["L0_tok_pos_embedding"].reshape(NEMB, D)
    pos_rows = pos[1 + np.arange(ET * P) % NPATCH].reshape(ET, P, D).transpose(1, 0, 2)
    small = np.concatenate([a["L0_tok_proj_b"], a["L0_tok_cls_token"].reshape(D), pos[0]])[None]

    def heads_apart(m):
        out = np.zeros((m.shape[0], LOFF), f32)
        for part in range(2):
            to = out[:, part * QG:(part + 1) * QG].reshape(-1, NG, NJ, 32)
            to[:, :, :, 0:HD] = m[:, part * D:(part + 1) * D].reshape(-1, NG, NJ, HD)
        out[:, VOFF:] = m[:, 2 * D:]
        return out

    wa = np.zeros((2 * P, NWA), f32)
    wa[0:D, 0:LOFF] = heads_apart(a["L0_attn_qkv_w"].T)
    wa[D:, 0:LOFF] = heads_apart(a["L0_attn_lora_b"].reshape(E * R, 3 * D))
    wa[0:D, LOFF:LOFF + E * R] = a["L0_attn_lora_a"].transpose(1, 0, 2).reshape(D, E * R)
    wa[0:D, LOFF + E * R:] = a["L0_attn_gate_w"].T
    wa = wa.reshape(2, P, NWA).transpose(1, 0, 2)
    bias = heads_apart(a["L0_attn_qkv_b"][None])[0]
    bqk = bias[0:VOFF].reshape(2 * NG, P).T
    bv = np.broadcast_to(bias[VOFF:], (N, D))
    out_w = np.zeros((DC + 1, 2, D), f32)
    for c in range(2):
        out_w[0:DC, c] = a["L0_attn_proj_w"].T[c * DC:(c + 1) * DC]
    out_w[DC, 1] = a["L0_attn_proj_b"]
    gate_w = a["L0_ffn_gate_w"].reshape(2, DC, E).transpose(1, 0, 2)

    p = np.arange(P)
    consts = np.zeros((P, C_ALL), f32)
    consts[:, C_ID:C_ID + P] = np.eye(P)
    consts[:, C_TRI:C_TRI + N] = p[:, None] < np.arange(N)[None, :]
    consts[:, C_ONE:C_ONE + P] = 1
    consts[:, C_IOTA:C_IOTA + GE] = np.tile(np.arange(E) - E, GB)
    consts[:, C_J:C_J + E * MOST] = np.tile(P * np.arange(MOST), E)
    consts[:, C_T:C_T + LOADS * E] = np.repeat(np.arange(LOADS), E)
    consts[:, C_TT:C_TT + LOADS] = np.arange(LOADS)
    consts[:, C_POW:C_POW + 3] = (-0.5, 0.5, EPS)
    consts[:, C_TOK:C_TOK + B] = N * np.arange(B)[None, :] + p[:, None]
    consts[:, C_FILL] = T + p
    consts[:, C_REG:C_REG + E] = REGION * np.arange(E)
    consts[:, C_BIAS:C_BIAS + GE] = np.tile(a["L0_ffn_gate_bias"], GB)

    nc = bacc.Bacc("TRN2", target_bir_lowering=False, num_devices=1)
    arrays = {
        "patches": patches, "txt": a["txt"], "proj_w": proj_w, "pos_rows": pos_rows, "small": small, "wa": wa,
        "bqk": bqk, "bv": bv, "out_w": out_w, "gate_w": gate_w, "consts": consts, "w1": a["L0_ffn_w1"],
        "w2": a["L0_ffn_w2"], "w3": a["L0_ffn_w3"], "w1s": a["L0_ffn_w1s"], "w2s": a["L0_ffn_w2s"], "w3s": a["L0_ffn_w3s"],
    }
    arrays = {f"in_{k}": np.ascontiguousarray(v) for k, v in arrays.items()}
    args = [nc.dram_tensor(k, v.shape, _mybir.dt.from_np(v.dtype), kind="ExternalInput").ap() for k, v in arrays.items()]
    args.append(nc.dram_tensor("acc", (T + P, D), F32, kind="ExternalOutput").ap())
    args.append(nc.dram_tensor("xs", (E * REGION + SPARE * P, ROW), F32, kind="Internal").ap())
    args.append(nc.dram_tensor("emb", (B * NPATCH, D), F32, kind="Internal").ap())
    program(nc, *args)
    r = run(nc, [arrays], core_ids=[0])
    return r.results[0]["acc"][0:T].reshape(B, N, D)
```
